# Optimizing a Trainium2 kernel written in Bass

```python
import numpy as np
import jax
import jax.numpy as jnp

def _softmax(x, axis=-1):
    return jax.nn.softmax(x, axis=axis)

def _gelu(x):
    return jax.nn.gelu(x, approximate=True)

def _silu(x):
    return jax.nn.silu(x)

def _sigmoid(x):
    return jax.nn.sigmoid(x)

def _layernorm(x, axis=-1, eps=1e-05):
    m = jnp.mean(x, axis=axis, keepdims=True)
    v = jnp.var(x, axis=axis, keepdims=True)
    return (x - m) / jnp.sqrt(v + eps)

def _scatter_add(tgt, idx, src, axis=0):
    return tgt.at[idx].add(src)

def _segment_sum(src, seg, n):
    return jax.ops.segment_sum(src, seg, n)
kernel_name = 'mk_flamingo_gated_d2_seqx_r8_9cfdcd'

def setup_inputs(seed: int=0):
    np.random.seed(seed)
    _w = jnp.asarray

    def _rec_inputs():
        import jax
        import jax.numpy as jnp
        _rk = jax.random.key(seed)
        x = 7.22e-05 + 1 * jax.random.normal(jax.random.fold_in(_rk, 1), (16, 128, 256), jnp.float32)
        _lenS = 128 - jax.random.randint(jax.random.fold_in(_rk, 7), (16,), 0, max(1, 128 // 4) + 1, jnp.int32)
        _lenS2 = 128 - jax.random.randint(jax.random.fold_in(_rk, 8), (16,), 0, max(1, 128 // 4) + 1, jnp.int32)
        _ctx_512P = jax.random.normal(jax.random.fold_in(_rk, 11), (16, 16, 64), jnp.float32)
        _ctx_512c = jax.random.dirichlet(jax.random.fold_in(_rk, 511), 0.3 * jnp.ones((16,), jnp.float32), (16, 128))
        _ctx_512t = jnp.einsum('bsk,bkd->bsd', _ctx_512c, _ctx_512P)
        _ctx_512t = _ctx_512t * jax.lax.rsqrt(jnp.mean(jnp.square(_ctx_512t)) + 1e-12) * 0.953939
        ctx_512 = -0.000514642 + 1.00011 * (_ctx_512t + 0.3 * jax.random.normal(jax.random.fold_in(_rk, 611), (16, 128, 64), jnp.float32))
        _g = jax.random.normal(jax.random.fold_in(_rk, 9001), (2, 2), jnp.float32)
        _g = jnp.sign(_g) * jnp.maximum(jnp.abs(_g), 1.0) + (_g == 0) * 1.0
        g_xattn = _g[0]
        g_ffn = _g[1]
        return (x, ctx_512, g_xattn, g_ffn)
    x, ctx_512, g_xattn, g_ffn = _rec_inputs()

    def _L0_xattn_setup():
        import jax, jax.numpy as jnp
        import numpy as np
        import math
        D_MODEL = 256
        N_HEADS = 16
        N_GROUPS = 4
        HEADS_PER_GROUP = N_HEADS // N_GROUPS
        HEAD_DIM = D_MODEL // N_HEADS
        B, S = (2, 256)
        key = jax.random.key(seed)
        k1, k2, k3, k4, k5 = jax.random.split(key, 5)
        q = jax.random.normal(k1, (B, S, D_MODEL), dtype=jnp.float32)
        k = jax.random.normal(k2, (B, S, N_GROUPS * HEAD_DIM), dtype=jnp.float32)
        v = jax.random.normal(k3, (B, S, N_GROUPS * HEAD_DIM), dtype=jnp.float32)
        lim = 1.0 / math.sqrt(D_MODEL)
        Wc = jax.random.uniform(k4, (D_MODEL, D_MODEL), minval=-lim, maxval=lim, dtype=jnp.float32)
        bc = jax.random.uniform(k5, (D_MODEL,), minval=-lim, maxval=lim, dtype=jnp.float32)
        return {'q': q, 'k': k, 'v': v, 'Wc': Wc, 'bc': bc}
    _L0_xattn_all = _L0_xattn_setup()
    _L0_xattn_in = {k: v for k, v in _L0_xattn_all.items() if k in ('Wc', 'bc')}
    del _L0_xattn_all

    def _L0_ffn_setup():
        import jax, jax.numpy as jnp
        import numpy as np

        def _sparsify_2to4(h):
            B, S, I = h.shape
            g = h.reshape(B, S, I // 4, 4)
            a = jnp.abs(g)
            _, idx = jax.lax.top_k(a, 2)
            pos = jnp.arange(4)
            mask = (pos == idx[..., 0:1]) | (pos == idx[..., 1:2])
            return (g * mask.astype(g.dtype)).reshape(B, S, I)
        key = jax.random.key(seed)
        k1, k2, k3, k4 = jax.random.split(key, 4)
        B, S, H, I = (4, 256, 256, 1024)
        x = jax.random.normal(k1, (B, S, H), dtype=jnp.float32)
        w_gate = jax.random.normal(k2, (H, I), dtype=jnp.float32) / np.sqrt(H)
        w_up = jax.random.normal(k3, (H, I), dtype=jnp.float32) / np.sqrt(H)
        w_down = jax.random.normal(k4, (I, H), dtype=jnp.float32) / np.sqrt(I)
        return {'x': x, 'w_gate': w_gate, 'w_up': w_up, 'w_down': w_down}
    _L0_ffn_all = _L0_ffn_setup()
    _L0_ffn_in = {k: v for k, v in _L0_ffn_all.items() if k in ('w_gate', 'w_up', 'w_down')}
    del _L0_ffn_all

    def _L1_xattn_setup():
        import jax, jax.numpy as jnp
        import numpy as np
        import math
        NUM_Q_HEADS = 32
        NUM_KV_HEADS = 8
        key = jax.random.key(seed)
        k1, k2, k3 = jax.random.split(key, 3)
        B, S, E = (2, 256, 256)
        kv_E = NUM_KV_HEADS * (E // NUM_Q_HEADS)
        q = jax.random.normal(k1, (B, S, E), dtype=jnp.float32)
        k = jax.random.normal(k2, (B, S, kv_E), dtype=jnp.float32)
        v = jax.random.normal(k3, (B, S, kv_E), dtype=jnp.float32)
        return {'q': q, 'k': k, 'v': v}
    _L1_xattn_all = _L1_xattn_setup()
    _L1_xattn_in = {k: v for k, v in _L1_xattn_all.items() if k in ()}
    del _L1_xattn_all

    def _L1_ffn_setup():
        import jax, jax.numpy as jnp
        import numpy as np
        B, S, DIM = (2, 256, 256)
        INTER = 176
        E = 8
        K = 2
        SHARED = 1
        ROUTE_SCALE = 1.0

        def _expert(xt, w1, w2, w3, cw=None):
            h = jax.nn.silu((xt @ w1.T).astype(jnp.float32)) * (xt @ w3.T).astype(jnp.float32)
            if cw is not None:
                h = cw[:, None] * h
            return h.astype(xt.dtype) @ w2.T
        key = jax.random.key(seed)
        ks = jax.random.split(key, 9)
        bf = lambda k, shape: (jax.random.normal(k, shape, dtype=jnp.float32) * 0.02).astype(jnp.bfloat16)
        return {'x': jax.random.normal(ks[0], (B, S, DIM), dtype=jnp.float32).astype(jnp.bfloat16), 'gate_w': jax.random.normal(ks[1], (E, DIM), dtype=jnp.float32) * 0.02, 'gate_b': jax.random.normal(ks[2], (E,), dtype=jnp.float32) * 0.01, 'w1': bf(ks[3], (E, INTER, DIM)), 'w2': bf(ks[4], (E, DIM, INTER)), 'w3': bf(ks[5], (E, INTER, DIM)), 'sw1': bf(ks[6], (SHARED * INTER, DIM)), 'sw2': bf(ks[7], (DIM, SHARED * INTER)), 'sw3': bf(ks[8], (SHARED * INTER, DIM))}
    _L1_ffn_all = _L1_ffn_setup()
    _L1_ffn_in = {k: v for k, v in _L1_ffn_all.items() if k in ('gate_w', 'gate_b', 'w1', 'w2', 'w3', 'sw1', 'sw2', 'sw3')}
    del _L1_ffn_all
    return {'x': x, 'ctx_512': ctx_512, 'g_xattn': g_xattn, 'g_ffn': g_ffn, 'L0_xattn_Wc': _L0_xattn_in['Wc'], 'L0_xattn_bc': _L0_xattn_in['bc'], 'L0_ffn_w_gate': _L0_ffn_in['w_gate'], 'L0_ffn_w_up': _L0_ffn_in['w_up'], 'L0_ffn_w_down': _L0_ffn_in['w_down'], 'L1_ffn_gate_w': _L1_ffn_in['gate_w'], 'L1_ffn_gate_b': _L1_ffn_in['gate_b'], 'L1_ffn_w1': _L1_ffn_in['w1'], 'L1_ffn_w2': _L1_ffn_in['w2'], 'L1_ffn_w3': _L1_ffn_in['w3'], 'L1_ffn_sw1': _L1_ffn_in['sw1'], 'L1_ffn_sw2': _L1_ffn_in['sw2'], 'L1_ffn_sw3': _L1_ffn_in['sw3']}

def reference(x, ctx_512, g_xattn, g_ffn, L0_xattn_Wc, L0_xattn_bc, L0_ffn_w_gate, L0_ffn_w_up, L0_ffn_w_down, L1_ffn_gate_w, L1_ffn_gate_b, L1_ffn_w1, L1_ffn_w2, L1_ffn_w3, L1_ffn_sw1, L1_ffn_sw2, L1_ffn_sw3):
    import jax
    import jax.numpy as jnp

    def _L0_xattn_ref(q, k, v, Wc, bc):
        import jax, jax.numpy as jnp
        import numpy as np
        import math
        D_MODEL = 256
        N_HEADS = 16
        N_GROUPS = 4
        HEADS_PER_GROUP = N_HEADS // N_GROUPS
        HEAD_DIM = D_MODEL // N_HEADS
        B, S = (2, 256)
        b, s, _ = q.shape
        qh = q.reshape(b, s, N_GROUPS, HEADS_PER_GROUP, HEAD_DIM).transpose(0, 2, 3, 1, 4)
        kh = k.reshape(b, s, N_GROUPS, HEAD_DIM).transpose(0, 2, 1, 3)
        vh = v.reshape(b, s, N_GROUPS, HEAD_DIM).transpose(0, 2, 1, 3)
        scale = 1.0 / math.sqrt(HEAD_DIM)
        scores = jnp.einsum('bghsd,bgtd->bghst', qh, kh) * scale
        probs = jax.nn.softmax(scores, axis=-1)
        out = jnp.einsum('bghst,bgtd->bghsd', probs, vh)
        out = out.transpose(0, 3, 1, 2, 4).reshape(b, s, D_MODEL)
        return out @ Wc.T + bc

    def _L0_ffn_ref(x, w_gate, w_up, w_down):
        import jax, jax.numpy as jnp
        import numpy as np

        def _sparsify_2to4(h):
            B, S, I = h.shape
            g = h.reshape(B, S, I // 4, 4)
            a = jnp.abs(g)
            _, idx = jax.lax.top_k(a, 2)
            pos = jnp.arange(4)
            mask = (pos == idx[..., 0:1]) | (pos == idx[..., 1:2])
            return (g * mask.astype(g.dtype)).reshape(B, S, I)
        h = jax.nn.silu(jnp.einsum('bsh,hi->bsi', x, w_gate)) * jnp.einsum('bsh,hi->bsi', x, w_up)
        h_sparse = _sparsify_2to4(h)
        return jnp.einsum('bsi,ih->bsh', h_sparse, w_down)

    def _L1_xattn_ref(q, k, v):
        import jax, jax.numpy as jnp
        import numpy as np
        import math
        NUM_Q_HEADS = 32
        NUM_KV_HEADS = 8
        B, S, E = q.shape
        H, KV = (NUM_Q_HEADS, NUM_KV_HEADS)
        D = E // H
        G = H // KV
        scale = math.sqrt(D)
        qh = q.reshape(B, S, KV, G, D).transpose(0, 2, 3, 1, 4)
        kh = k.reshape(B, S, KV, D).transpose(0, 2, 1, 3)
        vh = v.reshape(B, S, KV, D).transpose(0, 2, 1, 3)
        scores = jnp.einsum('bkgsd,bktd->bkgst', qh, kh) / scale
        weights = jax.nn.softmax(scores, axis=-1)
        out = jnp.einsum('bkgst,bktd->bkgsd', weights, vh)
        return out.transpose(0, 3, 1, 2, 4).reshape(B, S, E)

    def _L1_ffn_ref(x, gate_w, gate_b, w1, w2, w3, sw1, sw2, sw3):
        import jax, jax.numpy as jnp
        import numpy as np
        B, S, DIM = (2, 256, 256)
        INTER = 176
        E = 8
        K = 2
        SHARED = 1
        ROUTE_SCALE = 1.0

        def _expert(xt, w1, w2, w3, cw=None):
            h = jax.nn.silu((xt @ w1.T).astype(jnp.float32)) * (xt @ w3.T).astype(jnp.float32)
            if cw is not None:
                h = cw[:, None] * h
            return h.astype(xt.dtype) @ w2.T
        Bx, Sx, D = x.shape
        xt = x.reshape(-1, D)
        T = xt.shape[0]
        scores = xt.astype(jnp.float32) @ gate_w.T
        scores = jnp.sqrt(jax.nn.softplus(scores))
        biased = scores + gate_b
        _, idx = jax.lax.top_k(biased, K)
        weights = jnp.take_along_axis(scores, idx, axis=1) * ROUTE_SCALE
        cw = jnp.einsum('tk,tke->te', weights, jax.nn.one_hot(idx, E, dtype=jnp.float32))
        y = jnp.zeros((T, D), dtype=xt.dtype)
        for e in range(E):
            y = y + _expert(xt, w1[e], w2[e], w3[e], cw[:, e])
        z = _expert(xt, sw1, sw2, sw3)
        return (y + z).reshape(Bx, Sx, D)
    x = x + jnp.tanh(g_xattn[0]) * _L0_xattn_ref(_layernorm(x, axis=-1), ctx_512, ctx_512, L0_xattn_Wc, L0_xattn_bc)
    x = x + jnp.tanh(g_ffn[0]) * _L0_ffn_ref(_layernorm(x, axis=-1), L0_ffn_w_gate, L0_ffn_w_up, L0_ffn_w_down)
    x = x + jnp.tanh(g_xattn[1]) * _L1_xattn_ref(_layernorm(x, axis=-1), ctx_512, ctx_512)
    x = x + jnp.tanh(g_ffn[1]) * _L1_ffn_ref(_layernorm(x, axis=-1), L1_ffn_gate_w, L1_ffn_gate_b, L1_ffn_w1, L1_ffn_w2, L1_ffn_w3, L1_ffn_sw1, L1_ffn_sw2, L1_ffn_sw3)
    return x

_drawn_inputs = setup_inputs


def setup_inputs(seed=0):
    import zlib

    import numpy as np

    out = dict(_drawn_inputs(seed))
    spreads = {'g_ffn': (-1.0, 0.6)}
    factors = {'L1_ffn_gate_w': 4.297,
     'L1_ffn_gate_b': 8.0,
     'L1_ffn_w1': 3.741,
     'L1_ffn_w2': 3.654,
     'L1_ffn_w3': 3.664,
     'L1_ffn_sw1': 5.124,
     'L1_ffn_sw2': 5.081,
     'L1_ffn_sw3': 5.065}
    for name, (base, spread) in spreads.items():
        noise = np.random.default_rng([zlib.crc32(name.encode()), seed]).standard_normal(out[name].shape)
        drawn = base * np.exp(spread * noise) if base else spread * noise
        out[name] = jnp.asarray(drawn.astype(out[name].dtype))
    for name, factor in factors.items():
        out[name] = (out[name] * factor).astype(out[name].dtype)
    return out
```

```python
from contextlib import ExitStack

import numpy as np

import concourse.bass as bass
from concourse import mybir

ALU = mybir.AluOpType
ACT = mybir.ActivationFunctionType
F32 = mybir.dt.float32
F32R = mybir.dt.float32r
BF16 = mybir.dt.bfloat16
AX = mybir.AxisListType



def flamingo_block(nc, x, ctx_kv, ctx_t, g_x, g_f, wc_t, bc, w_up, w_down, gate_w_t, gate_b, w13, w2, out):
    B, T, D = x.shape
    C = ctx_kv.shape[2]
    P = 128
    assert T == P and D == 2 * P and C == 64
    KT = D // P
    G0, HD0 = 4, 16
    G1, HD1 = 8, 8
    HPG = 4
    BLK = 32
    I0 = w_down.shape[0]
    E = gate_b.shape[0]
    EI = 176
    I1 = (E + 1) * EI
    NT1 = -(-I1 // P)
    PAIR = 2 * EI
    SH = 2 * EI + E
    EPS = 1e-5
    RND = B // 2
    assert I0 == 8 * P and E == 8

    ctx = ExitStack()
    with ctx:
        def sb(name, shape, dt=F32):
            return ctx.enter_context(nc.sbuf_tensor(name, shape, dt))

        def sem(name):
            return ctx.enter_context(nc.semaphore(name))

        up_hi = sb("up_hi", [P, KT, 2 * I0], F32R)
        up_lo = sb("up_lo", [P, KT, 2 * I0], F32R)
        down_hi = sb("down_hi", [P, I0 // P, D], F32R)
        down_lo = sb("down_lo", [P, I0 // P, D], F32R)
        wc_hi = sb("wc_hi", [P, KT, D], F32R)
        wc_lo = sb("wc_lo", [P, KT, D], F32R)
        w13_r = sb("w13_r", [P, KT, 2 * I1], F32R)
        gate_hi = sb("gate_hi", [P, KT, E], F32R)
        gate_lo = sb("gate_lo", [P, KT, E], F32R)
        w2_r = sb("w2_r", [P, NT1, D], F32R)
        gate_raw = sb("gate_raw", [P, KT, E])
        gb = sb("gb", [P, E])
        bcg = sb("bcg", [P, D])
        graw = sb("graw", [P, 4])
        tg = sb("tg", [P, 4])
        ident = sb("ident", [P, P])
        neg_half = sb("neg_half", [P, 1])
        half = sb("half", [P, E])
        tie = sb("tie", [P, 2, E, E], BF16)

        x0 = [sb(f"x0_{s}", [P, D]) for s in range(2)]
        xb = [sb(f"xb_{s}", [P, D]) for s in range(2)]
        x1 = [sb(f"x1_{s}", [P, D]) for s in range(2)]
        x2 = [sb(f"x2_{s}", [P, D]) for s in range(2)]
        x3 = [sb(f"x3_{s}", [P, D]) for s in range(2)]
        y = [sb(f"y_{s}", [P, D]) for s in range(2)]
        ct = [sb(f"ct_{s}", [P, C]) for s in range(2)]
        v0 = [sb(f"v0_{s}", [P, G0, BLK]) for s in range(2)]
        v1 = [sb(f"v1_{s}", [P, G1, BLK]) for s in range(2)]
        k0a = [sb(f"k0a_{s}", [P, G0, T], F32R) for s in range(2)]
        k0b = [sb(f"k0b_{s}", [P, G0, T], F32R) for s in range(2)]
        k1 = [sb(f"k1_{s}", [P, G1, T], F32R) for s in range(2)]

        a_stat = sb("a_stat", [P, 6])
        a_mv = sb("a_mv", [P, 2])
        a_ve = sb("a_ve", [P, 1])
        a_rs = sb("a_rs", [P, 1])
        a_xn = sb("a_xn", [P, D])
        q0a = sb("q0a", [P, HPG, G0, BLK])
        q0b = sb("q0b", [P, HPG, G0, BLK])
        q1 = sb("q1", [P, HPG, G1, BLK])
        qt0a = sb("qt0a", [P, HPG * T], F32R)
        qt0b = sb("qt0b", [P, HPG * T], F32R)
        qt1 = sb("qt1", [P, 2, HPG * T], F32R)
        pt = sb("pt", [P, G1, HPG * T])
        ot = sb("ot", [P, 2, HPG * T])
        rec = sb("rec", [P, HPG, G1])
        on = sb("on", [P, D])
        ao_hi = sb("ao_hi", [P, KT, P], F32R)
        ao_lo = sb("ao_lo", [P, KT, P], F32R)

        f_stat = sb("f_stat", [P, 6])
        f_mv = sb("f_mv", [P, 2])
        f_ve = sb("f_ve", [P, 1])
        f_rs = sb("f_rs", [P, 1])
        f_xn = sb("f_xn", [P, D])
        at_hi = sb("at_hi", [P, KT, P], F32R)
        at_lo = sb("at_lo", [P, KT, P], F32R)
        HW = NT1 * P
        work = sb("work", [P, 4 * 1024])
        hid = work[:, 0:HW]
        sg = work[:, HW:2 * HW]
        ht_hi = sb("ht_hi", [P, NT1, P], F32R)
        ht_lo = sb("ht_lo", [P, NT1, P], F32R)
        CH = 512
        NG = CH // 4
        pmax = sb("pmax", [P, NG, 2])
        pmin = sb("pmin", [P, NG, 2])
        lose = sb("lose", [P, NG, 2, 2], BF16)
        both = sb("both", [P, 2, NG], BF16)
        lead = sb("lead", [P, NG, 2], BF16)
        keep = sb("keep", [P, 2, CH], BF16)
        lg = sb("lg", [P, E])
        rt = sb("rt", [P, 10, E])
        cmp = sb("cmp", [P, 2, E, E], BF16)
        rank = sb("rank", [P, E])
        cw = sb("cw", [P, E])

        bank = [[ctx.enter_context(nc.psum_tensor(f"bank{s}{b}", [P, 512], F32)) for b in range(4)]
                for s in range(2)]

        kd0a = nc.dram_tensor("kd0a", (G0, 2, HD0, B * T), F32, kind="Internal").ap()
        kd0b = nc.dram_tensor("kd0b", (G0, HD0, B * T), F32, kind="Internal").ap()
        kd1 = nc.dram_tensor("kd1", (G1, 3, HD1, B * T), F32, kind="Internal").ap()

        names = """
        ld_kt ld_small ld_up ld_down ld_wc ld_w13 ld_w2 scratch_kd
        c_mem c_sel c_oh c_tg c_hi c_kh c_kl c_lo c_vec
        xb_done v0_done v1_done
        a_stats a_mvd a_veps a_rstd a_norm a_q_hi a_q_hi2 a_q_lo a_qt_ps a_qt_ps2 a_qt a_qt2
        a_m a_r a_mt_ps a_mt_ps2 a_mt a_mt2 a_mclear a_s a_e
        a_pv a_pv2 a_ot a_ot2 a_otT a_otT2 a_rec a_rec2 a_on a_on2 a_onT a_aohi a_aolo a_proj a_out
        f_stats f_mvd f_veps f_rstd f_norm f_xt_ps f_at_hi f_at_lo
        f_g0 f_u0 f_g1 f_u1 f_sg0 f_sg1 f_h0 f_h1 f_g2 f_u2 f_g3 f_u3 f_sg2 f_sg3 f_h2 f_h3
        f_abs0 f_abs1 f_pairs f_cmp f_lead f_cmp2 f_cmp3 f_rank f_keep0 f_keep1 f_hm0 f_hm1
        f_sh f_lg f_sgs f_hs f_r0 f_r1 f_r2 f_r3 f_r4 f_r5 f_r6 f_r7 f_r8 f_r9 f_r10 f_r11 f_cw
        f_t0 f_t1 f_t2 f_t3 f_th0 f_th1 f_th2 f_th3 f_tl0 f_tl1 f_tl2 f_tl3 f_y f_out
        """.split()
        S = {n: sem(n) for n in names}
        ld_x = [sem(f"ld_x{s}") for s in range(2)]
        ld_ct = [sem(f"ld_ct{s}") for s in range(2)]
        ld_k0 = [sem(f"ld_k0{s}") for s in range(2)]
        ld_k1 = [sem(f"ld_k1{s}") for s in range(2)]
        st_y = [sem(f"st_y{s}") for s in range(2)]

        def wait(eng, name, n):
            eng.wait_ge(S[name], n + 1)

        def wait_before(eng, name, n, back=1):
            if not (isinstance(n, int) and n < back):
                eng.wait_ge(S[name], n + 1 - back)

        def wait_part(eng, name, n, k):
            eng.wait_ge(S[name], 8 * n + k)

        def wait_alone(eng, name, n, back=0):
            if isinstance(n, int) and n < back:
                return
            count = n + 1 - back
            if not isinstance(count, int):
                count = eng.snap(eng.to_reg(count))
            eng.wait_ge(S["c_mem"], 13)
            eng.wait_ge(S[name], count)

        STEPS = 16

        def alternate(*phases):
            at = {ph: next(ph) for ph in phases}
            for step in range(STEPS):
                for ph in phases:
                    while at[ph] is not None and at[ph] <= step:
                        at[ph] = next(ph, None)

        def rounds(eng, attention, ffn, weights=None):
            def body(p):
                before = [] if isinstance(p, int) and p == 0 else [ffn(p - 1, 1, 1)]
                alternate(attention(p, 0, 0), *before)
                if weights and not before:
                    weights()
                alternate(attention(p, 1, 0), ffn(p, 0, 0))
                alternate(attention(p, 0, 1), ffn(p, 1, 0))
                alternate(attention(p, 1, 1), ffn(p, 0, 1))

            body(0)
            with eng.Fori(1, RND) as p:
                body(p)
            alternate(ffn(RND - 1, 1, 1))

        block = ctx.enter_context(nc.Block())
        G = [G0, G1]
        HD = [HD0, HD1]

        @block.sync
        def _(sp):
            kt_raw = work[0:C, 0:B * T]
            sp.dma_start(kt_raw, ctx_t).then_inc(S["ld_kt"], 16)
            sp.dma_start(graw[:, 0:2], g_x.partition_broadcast(P)).then_inc(S["ld_small"], 16)
            sp.dma_start(graw[:, 2:4], g_f.partition_broadcast(P)).then_inc(S["ld_small"], 16)
            sp.dma_start(bcg[:, :], bc.partition_broadcast(P)).then_inc(S["ld_small"], 16)
            sp.dma_start(gb[:, :], gate_b.partition_broadcast(P)).then_inc(S["ld_small"], 16)
            sp.dma_start(gate_raw[:, :, :], gate_w_t.rearrange("(k p) e -> p k e", p=P)).then_inc(S["ld_small"], 16)

            def load_x(i, s):
                sp.dma_start(x0[s][:, :], x[i]).then_inc(ld_x[s], 16)
                sp.dma_start(ct[s][:, :], ctx_kv[i]).then_inc(ld_ct[s], 16)

            def load_k0(i, s):
                for g in range(G0):
                    sp.dma_start(k0a[s][BLK * g:BLK * (g + 1), g, :].bitcast(F32),
                                 kd0a[g].rearrange("a d (b t) -> (a d) b t", t=T)[:, i, :]).then_inc(ld_k0[s], 16)
                    sp.dma_start(k0b[s][BLK * g:BLK * g + HD0, g, :].bitcast(F32),
                                 kd0b[g].rearrange("d (b t) -> d b t", t=T)[:, i, :]).then_inc(ld_k0[s], 16)

            def load_k1(i, s):
                for g in range(G1):
                    r = BLK * (g % 4)
                    sp.dma_start(k1[s][r:r + 3 * HD1, g, :].bitcast(F32),
                                 kd1[g].rearrange("a d (b t) -> (a d) b t", t=T)[:, i, :]).then_inc(ld_k1[s], 16)

            for s in range(2):
                load_x(s, s)
            sp.wait_ge(S["scratch_kd"], 16 * (2 * G0 + 1 + 3 * G1))
            sp.wait_ge(S["c_oh"], 3 * 2)
            for s in range(2):
                load_k0(s, s)
            for s in range(2):
                load_k1(s, s)

            def reload_attention_0(p, s):
                i, n = 2 * p + s, 4 * p + s
                wait(sp, "a_norm", n)
                wait(sp, "xb_done", i)
                wait(sp, "v1_done", i)
                wait(sp, "v0_done", i)
                load_x(i + 2, s)
                wait_part(sp, "a_s", n, 8)
                load_k0(i + 2, s)

            def reload_attention_1(p, s):
                wait_part(sp, "a_s", 4 * p + s + 2, 8)
                load_k1(2 * p + s + 2, s)

            def store(p, s):
                wait(sp, "f_out", 4 * p + s + 2)
                sp.dma_start(out[2 * p + s], y[s][:, :]).then_inc(st_y[s], 16)

            def body(p, last=False):
                if not (isinstance(p, int) and p == 0):
                    store(p - 1, 1)
                if not last:
                    for s in range(2):
                        reload_attention_0(p, s)
                    for s in range(2):
                        reload_attention_1(p, s)
                store(p, 0)

            body(0)
            with sp.Fori(1, RND - 1) as p:
                body(p)
            body(RND - 1, last=True)
            store(RND - 1, 1)
            for s in range(2):
                sp.wait_ge(st_y[s], 16 * RND)

        @block.gpsimd
        def _(pool):
            for t in (q0a, q0b, q1):
                pool.memset(t[:, :, :, :], 0.0).then_inc(S["c_mem"], 1)
            for t in (pt[:, 0:4, :], w2_r[:, NT1 - 1, :].bitcast(F32)):
                pool.memset(t, 0.0).then_inc(S["c_mem"], 1)
            for t in (v0[0], v0[1], v1[0], v1[1]):
                pool.memset(t[:, :, :], 0.0).then_inc(S["c_mem"], 1)
            pool.memset(ident[:, :], 0.0).then_inc(S["c_mem"], 1)
            pool.memset(neg_half[:, :], -0.5).then_inc(S["c_mem"], 1)
            pool.memset(half[:, :], 0.5).then_inc(S["c_mem"], 1)
            pool.memset(tie[:, :, :, :], 0.0).then_inc(S["c_mem"], 1)
            pool.wait_ge(S["c_mem"], 13)
            pool.dma_start(w13_r[:, :, :], w13.rearrange("(k p) n -> p k n", p=P)).then_inc(S["ld_w13"], 16)
            full = (NT1 - 1) * P
            pool.dma_start(w2_r[:, 0:NT1 - 1, :], w2[0:full].rearrange("(k p) n -> p k n", p=P)).then_inc(S["ld_w2"], 16)
            pool.dma_start(w2_r[0:I1 - full, NT1 - 1, :], w2[full:I1]).then_inc(S["ld_w2"], 16)
            pool.affine_select(out=ident[:, :], in_=ident[:, :], compare_op=ALU.not_equal, fill=1.0,
                               base=0, pattern=[[-1, P]], channel_multiplier=1).then_inc(S["c_sel"], 1)
            for half_, row in ((0, HD0), (2, 3 * HD1)):
                v = pt[:, half_, :].rearrange("p (g t) -> p g t", g=4)
                pool.affine_select(out=v, in_=v, compare_op=ALU.not_equal, fill=1.0, base=-row,
                                   pattern=[[-BLK, 4], [0, T]], channel_multiplier=1).then_inc(S["c_sel"], 1)
            for t, d in ((v0[0], HD0), (v0[1], HD0), (v1[0], HD1), (v1[1], HD1)):
                pool.memset(t[:, :, d:d + 1], 1.0).then_inc(S["c_sel"], 1)
            pool.affine_select(out=tie[:, 0], in_=tie[:, 0], compare_op=ALU.is_ge, fill=1.0,
                               base=0, pattern=[[-1, E], [1, E]], channel_multiplier=0).then_inc(S["c_sel"], 1)
            pool.affine_select(out=tie[:, 1], in_=tie[:, 1], compare_op=ALU.is_ge, fill=1.0,
                               base=0, pattern=[[1, E], [-1, E]], channel_multiplier=0).then_inc(S["c_sel"], 1)
            pool.wait_ge(S["c_vec"], 1)

            def rstd(pre, n, mv, ve, rs):
                wait_alone(pool, pre + "mvd", n)
                pool.tensor_scalar(ve[:, :], mv[:, 1:2], EPS, None, ALU.add).then_inc(S[pre + "veps"], 1)
                wait(pool, pre + "veps", n)
                pool.tensor_tensor(rs[:, :], ve[:, :], neg_half[:, :], ALU.pow).then_inc(S[pre + "rstd"], 1)

            def attention(p, s, L):
                yield 0
                n, i = 4 * p + s + 2 * L, 2 * p + s
                rstd("a_", n, a_mv, a_ve, a_rs)
                yield 1
                wait(pool, "a_q_hi", n)
                d = HD[L]
                q, qs = (q0a, q0a) if L == 0 else (q1, q1)
                xv = a_xn[:, :].rearrange("p (g j d) -> p j g d", g=G[L], j=HPG)
                for j in range(HPG):
                    last = pool.tensor_tensor(q[:, j, :, d:2 * d], xv[:, j], qs[:, j, :, 0:d], ALU.subtract)
                last.then_inc(S["a_q_lo"], 1)
                yield 2
                if L == 0:
                    pool.wait_ge(ld_x[s], 16 * (p + 1))
                    wait_before(pool, "a_out", n, 4)
                    pool.tensor_tensor(xb[s][:, :], x0[s][:, :], bcg[:, :], ALU.add).then_inc(S["xb_done"], 1)
                    wait_alone(pool, "a_pv", n, 4)
                    pool.wait_ge(ld_ct[s], 16 * (p + 1))
                    pool.tensor_copy(v0[s][:, :, 0:HD0], ct[s][:, :].rearrange("p (g d) -> p g d", g=G0))\
                        .then_inc(S["v0_done"], 1)
                    wait_alone(pool, "a_pv2", i, 2)
                    pool.tensor_copy(v1[s][:, :, 0:HD1], ct[s][:, :].rearrange("p (g d) -> p g d", g=G1))\
                        .then_inc(S["v1_done"], 1)
                else:
                    yield 7
                    wait_alone(pool, "a_mt_ps2", i)
                    pool.memset(q1[:, :, :, 3 * HD1:3 * HD1 + 1], 0.0).then_inc(S["a_mclear"], 1)

            def ffn(p, s, L):
                yield 0
                n, i = 4 * p + s + 2 * L, 2 * p + s
                rstd("f_", n, f_mv, f_ve, f_rs)
                if L == 0:
                    for c in range(2):
                        yield 5 + 3 * c
                        wait(pool, f"f_keep{c}", i)
                        h = hid[:, CH * c:CH * (c + 1)]
                        pool.tensor_tensor(h, h, keep[:, c, :], ALU.mult).then_inc(S[f"f_hm{c}"], 1)
                else:
                    yield 4
                    wait(pool, "f_r7", i)
                    pool.tensor_tensor(rt[:, 8, :], rt[:, 7, :], half[:, :], ALU.pow).then_inc(S["f_r8"], 1)

            rounds(pool, attention, ffn)

        @block.scalar
        def _(act):
            kt_raw = work[0:C, 0:B * T]
            act.dma_start(work[:, 2048:2048 + 2 * D].rearrange("p (k n) -> p k n", k=KT),
                          wc_t.rearrange("(k p) n -> p k n", p=P)).then_inc(S["ld_wc"], 16)
            kh = ht_hi[0:C, :, :].rearrange("p a b -> p (a b)")
            act.wait_ge(S["ld_kt"], 16)
            kh = up_lo[0:C, 0, 0:B * T]
            act.activation(kh, kt_raw, ACT.Copy).then_inc(S["c_kh"], 1)
            act.wait_ge(S["ld_small"], 16 * 5)
            act.activation(tg[:, :], graw[:, :], ACT.Tanh).then_inc(S["c_tg"], 1)
            act.activation(gate_hi[:, :, :], gate_raw[:, :, :], ACT.Copy).then_inc(S["c_hi"], 1)
            act.wait_ge(S["ld_wc"], 16)
            act.activation(wc_hi[:, :, :], work[:, 2048:2048 + 2 * D].rearrange("p (k n) -> p k n", k=KT), ACT.Copy)\
               .then_inc(S["c_hi"], 1)
            act.wait_ge(S["c_kh"], 1)
            for g in range(G0):
                for a in range(2):
                    act.dma_start(kd0a[g, a], kh[HD0 * g:HD0 * (g + 1), :].bitcast(F32)).then_inc(S["scratch_kd"], 16)
            for g in range(G1):
                for a in range(2):
                    act.dma_start(kd1[g, a], kh[HD1 * g:HD1 * (g + 1), :].bitcast(F32)).then_inc(S["scratch_kd"], 16)
            kl = up_lo[0:C, 1, 0:B * T]
            act.wait_ge(S["c_kl"], 1)
            act.dma_start(kd0b.rearrange("g d n -> (g d) n"), kl.bitcast(F32)).then_inc(S["scratch_kd"], 16)
            for g in range(G1):
                act.dma_start(kd1[g, 2], kl[HD1 * g:HD1 * (g + 1), :].bitcast(F32)).then_inc(S["scratch_kd"], 16)
            act.wait_ge(S["scratch_kd"], 16 * (2 * G0 + 1 + 3 * G1))
            act.wait_ge(S["c_lo"], 2)
            st_up = [work[:, 0:2048], work[:, 2048:4096]]
            for k in range(KT):
                act.dma_start(st_up[k], w_up[k * P:(k + 1) * P, :]).then_inc(S["ld_up"], 16)

            def round_ffn_0_weights():
                act.wait_ge(S["ld_up"], 32)
                for k in range(KT):
                    act.activation(up_hi[:, k, :], st_up[k], ACT.Copy).then_inc(S["c_hi"], 1)
                act.wait_ge(S["c_lo"], 4)
                st_down = work[:, 0:(I0 // P) * D].rearrange("p (k n) -> p k n", n=D)
                act.dma_start(st_down, w_down.rearrange("(k p) n -> p k n", p=P)).then_inc(S["ld_down"], 16)
                act.wait_ge(S["ld_down"], 16)
                act.activation(down_hi[:, :, :], st_down, ACT.Copy).then_inc(S["c_hi"], 1)

            def attention(p, s, L):
                yield 1
                n, i = 4 * p + s + 2 * L, 2 * p + s
                B_ = bank[s]
                d = HD[L]
                wait(act, "a_norm", n)
                xv = a_xn[:, :].rearrange("p (g j d) -> p j g d", g=G[L], j=HPG)
                if L == 0:
                    if not isinstance(p, int) or p + s > 0:
                        wait_before(act, "a_qt_ps", n, 1)
                    act.activation(q0a[:, :, :, 0:d].bitcast(F32R), xv, ACT.Copy).then_inc(S["a_q_hi"], 1)
                    act.activation(q0b[:, :, :, 0:d].bitcast(F32R), xv, ACT.Copy).then_inc(S["a_q_hi2"], 1)
                else:
                    act.activation(q1[:, :, :, 0:d].bitcast(F32R), xv, ACT.Copy).then_inc(S["a_q_hi"], 1)
                    act.activation(q1[:, :, :, 2 * d:3 * d].bitcast(F32R), xv, ACT.Copy).then_inc(S["a_q_hi2"], 1)
                yield 2
                wait(act, "a_qt_ps", n)
                if L == 0:
                    act.activation(qt0a[:, :], B_[0][:, :], ACT.Copy).then_inc(S["a_qt"], 1)
                else:
                    act.activation(qt1[:, 0, :], B_[0][:, :], ACT.Copy).then_inc(S["a_qt"], 1)
                    wait(act, "a_qt_ps2", i)
                    act.activation(qt1[:, 1, :], B_[1][:, :], ACT.Copy).then_inc(S["a_qt2"], 1)
                yield 7
                wait(act, "a_mt_ps", n)
                if L == 0:
                    act.activation(qt0b[:, :], B_[1][:, :], ACT.Copy).then_inc(S["a_mt"], 1)
                else:
                    act.activation(qt1[:, 0, :], B_[0][:, :], ACT.Copy).then_inc(S["a_mt"], 1)
                    wait(act, "a_mt_ps2", i)
                    act.activation(qt1[:, 1, :], B_[1][:, :], ACT.Copy).then_inc(S["a_mt2"], 1)
                step = 8 // G[L]
                for g in range(G[L]):
                    yield 8 + g // 2
                    wait_part(act, "a_s", n, step * (g + 1))
                    act.activation(pt[:, g, :], B_[(2 + g) % 4][:, :], ACT.Exp, scale=float(d) ** -0.5)\
                       .then_inc(S["a_e"], step)
                yield 12
                wait(act, "a_pv", n)
                act.activation(ot[:, 0, :], B_[2][:, :], ACT.Copy).then_inc(S["a_ot"], 1)
                if L == 1:
                    wait(act, "a_pv2", i)
                    act.activation(ot[:, 1, :], B_[3][:, :], ACT.Copy).then_inc(S["a_ot2"], 1)
                yield 14
                if L == 0:
                    wait(act, "a_onT", i)
                    act.activation(ao_hi[:, :, :], B_[0][:, 0:D].rearrange("p (k t) -> p k t", k=KT), ACT.Copy)\
                       .then_inc(S["a_aohi"], 1)

            def ffn(p, s, L):
                yield 1
                n, i = 4 * p + s + 2 * L, 2 * p + s
                B_ = bank[s]
                wait(act, "f_xt_ps", n)
                act.activation(at_hi[:, :, :], B_[0][:, 0:D].rearrange("p (k t) -> p k t", k=KT), ACT.Copy)\
                   .then_inc(S["f_at_hi"], 1)

                def hidden_t(t, b, cols):
                    wait(act, f"f_t{t}", i if t > 1 else n)
                    act.activation(ht_hi[:, 4 * t:4 * t + cols // P, :],
                                   B_[b][:, 0:cols].rearrange("p (k t) -> p k t", t=P), ACT.Copy)\
                       .then_inc(S[f"f_th{t}"], 1)

                if L == 0:
                    for c in range(2):
                        yield (3, 5)[c]
                        wait(act, f"f_g{c}", n)
                        act.activation(sg[:, CH * c:CH * (c + 1)], B_[(1, 3)[c]][:, :], ACT.Silu)\
                           .then_inc(S[f"f_sg{c}"], 1)
                        yield (4, 7)[c]
                        wait(act, f"f_h{c}", n)
                        act.activation(sg[:, CH * c:CH * (c + 1)], hid[:, CH * c:CH * (c + 1)], ACT.Abs)\
                           .then_inc(S[f"f_abs{c}"], 1)
                    for t, b in ((0, 1), (1, 3)):
                        yield (8, 11)[t]
                        hidden_t(t, b, 4 * P)
                else:
                    yield 3
                    wait(act, "f_r1", i)
                    act.activation(rt[:, 1, :], rt[:, 0, :], ACT.Exp).then_inc(S["f_r2"], 1)
                    yield 4
                    wait(act, "f_r3", i)
                    act.activation(rt[:, 3, :], rt[:, 2, :], ACT.Ln).then_inc(S["f_r4"], 1)
                    act.activation(sg[:, (E * EI):I1], B_[1][:, 0:EI], ACT.Silu).then_inc(S["f_sgs"], 1)
                    for q in range(4):
                        yield 5 + q
                        wait(act, f"f_g{q}", n if q < 2 else i)
                        act.activation(sg[:, PAIR * q:PAIR * (q + 1)], B_[(2, 0)[q % 2]][:, 0:PAIR], ACT.Silu)\
                           .then_inc(S[f"f_sg{q}"], 1)
                    for t, b in ((0, 2), (1, 3), (2, 0), (3, 1)):
                        yield 9 + t
                        hidden_t(t, b, 4 * P if t < 3 else P)

            rounds(act, attention, ffn, round_ffn_0_weights)

        @block.tensor
        def _(pe):
            pe.wait_ge(S["c_sel"], 9)
            pe.wait_ge(S["c_mem"], 13)

            def product(o, a_hi, a_lo, w_hi, w_lo, first, last, free=False):
                pe.matmul(o, a_hi, w_hi, start=first, stop=False, skip_group_check=free)
                if w_lo is not None:
                    pe.matmul(o, a_hi, w_lo, start=False, stop=False, skip_group_check=free)
                return pe.matmul(o, a_lo, w_hi, start=False, stop=last, skip_group_check=free)

            def turn(o, src, count):
                for k in range(count):
                    last = pe.transpose(o[:, P * k:P * (k + 1)], src(k), ident[:, :])
                return last

            def attention(p, s, L):
                yield 2
                n, i = 4 * p + s + 2 * L, 2 * p + s
                B_ = bank[s]
                q = q0a if L == 0 else q1
                tiles = G[L] // 4
                step = 8 // G[L]
                if L == 0:
                    wait_before(pe, "f_out", n, 2)
                else:
                    wait(pe, "f_out", n - 2)
                    wait_before(pe, "a_mclear", i)
                wait(pe, "a_q_hi", n)
                wait(pe, "a_q_lo", n)
                if L == 0:
                    turn(B_[0], lambda j: q0a[:, j].rearrange("p g b -> p (g b)"), HPG).then_inc(S["a_qt_ps"], 1)
                else:
                    wait(pe, "a_q_hi2", n)
                    turn(B_[0], lambda j: q1[:, j, 0:4].rearrange("p g b -> p (g b)"), HPG).then_inc(S["a_qt_ps"], 1)
                    turn(B_[1], lambda j: q1[:, j, 4:8].rearrange("p g b -> p (g b)"), HPG).then_inc(S["a_qt_ps2"], 1)
                yield 3
                k_ = (k0a if L == 0 else k1)[s]
                pe.wait_ge((ld_k0 if L == 0 else ld_k1)[s], 16 * 8 * (p + 1))
                wait(pe, "a_qt", n)
                if L == 1:
                    wait(pe, "a_qt2", i)
                order = [(j, t) for t in range(tiles) for j in range(HPG)]
                for m, (j, t) in enumerate(order):
                    yield 3 + m // 2
                    if m >= 4:
                        wait_part(pe, "a_r", n, step * (m - 3))
                    qt = qt0a[:, P * j:P * (j + 1)] if L == 0 else qt1[:, t, P * j:P * (j + 1)]
                    pe.matmul(B_[(1 + m) % 4 if L == 0 else (2 + m) % 4][:, :], qt,
                              k_[:, 4 * t:4 * t + 4, :].rearrange("p g t -> p (g t)"), start=True, stop=True)\
                      .then_inc(S["a_m"], step)
                yield 7
                wait_part(pe, "a_r", n, 8)
                if L == 0:
                    wait(pe, "a_q_hi2", n)
                    turn(B_[1], lambda j: q0b[:, j].rearrange("p g b -> p (g b)"), HPG).then_inc(S["a_mt_ps"], 1)
                else:
                    turn(B_[0], lambda j: q1[:, j, 0:4].rearrange("p g b -> p (g b)"), HPG).then_inc(S["a_mt_ps"], 1)
                    turn(B_[1], lambda j: q1[:, j, 4:8].rearrange("p g b -> p (g b)"), HPG).then_inc(S["a_mt_ps2"], 1)
                wait(pe, "a_mt", n)
                if L == 1:
                    wait(pe, "a_mt2", i)
                for g in range(G[L]):
                    yield 8 + g // 2
                    if g >= 4:
                        wait_part(pe, "a_e", n, step * (g - 3))
                    o = B_[(2 + g) % 4][:, :]
                    if L == 0:
                        pe.matmul(o, k0a[s][:, g, :], qt0a[:, :], start=True, stop=False)
                        last = pe.matmul(o, k0b[s][:, g, :], qt0b[:, :], start=False, stop=True)
                    else:
                        last = pe.matmul(o, k1[s][:, g, :], qt1[:, g // 4, :], start=True, stop=True)
                    last.then_inc(S["a_s"], step)
                yield 12
                wait(pe, "v0_done" if L == 0 else "v1_done", i)
                vv = (v0 if L == 0 else v1)[s]
                for t in range(tiles):
                    wait_part(pe, "a_e", n, 8 if L == 0 or t == 1 else 5)
                    for g in range(4):
                        last = pe.matmul(B_[2 + t][BLK * g:BLK * (g + 1), :], vv[:, 4 * t + g, :], pt[:, 4 * t + g, :],
                                         start=True, stop=True)
                    last.then_inc(S["a_pv" if t == 0 else "a_pv2"], 1)
                yield 13
                wait(pe, "a_ot", n)
                o = B_[3] if L == 0 else B_[0]
                if L == 1:
                    wait_part(pe, "a_e", n, 8)
                turn(o, lambda j: ot[:, 0, P * j:P * (j + 1)], HPG).then_inc(S["a_otT"], 1)
                if L == 1:
                    wait(pe, "a_ot2", i)
                    turn(B_[1], lambda j: ot[:, 1, P * j:P * (j + 1)], HPG).then_inc(S["a_otT2"], 1)
                yield 14
                if L == 0:
                    wait(pe, "a_on", n)
                    turn(B_[0], lambda k: on[:, P * k:P * (k + 1)], KT).then_inc(S["a_onT"], 1)
                    yield 15
                    wait(pe, "a_aohi", i)
                    wait(pe, "a_aolo", i)
                    if isinstance(p, int) and p == 0 and s == 0:
                        pe.wait_ge(S["c_hi"], 2)
                        pe.wait_ge(S["c_lo"], 2)
                    for k in range(KT):
                        last = product(B_[1][:, 0:D], ao_hi[:, k, :], ao_lo[:, k, :], wc_hi[:, k, :], wc_lo[:, k, :],
                                       k == 0, k == KT - 1)
                    last.then_inc(S["a_proj"], 1)

            def ffn(p, s, L):
                yield 1
                n, i = 4 * p + s + 2 * L, 2 * p + s
                B_ = bank[s]
                if isinstance(p, int) and p == 0 and s == 0:
                    if L == 0:
                        pe.wait_ge(S["c_hi"], 5)
                        pe.wait_ge(S["c_lo"], 5)
                    else:
                        pe.wait_ge(S["ld_w13"], 16)
                        pe.wait_ge(S["ld_w2"], 32)
                wait(pe, "a_out", n)
                wait(pe, "f_norm", n)
                turn(B_[0], lambda k: f_xn[:, P * k:P * (k + 1)], KT).then_inc(S["f_xt_ps"], 1)
                yield 2
                wait(pe, "f_at_hi", n)
                wait(pe, "f_at_lo", n)

                def down(ks, w_hi, w_lo, y_):
                    for k in ks:
                        last = product(y_[:, 0:D], ht_hi[:, k, :], ht_lo[:, k, :], w_hi[:, k, :],
                                       None if w_lo is None else w_lo[:, k, :], k == 0, k == (NT1 - 1 if L else 7))
                    return last

                if L == 0:
                    for c in range(2):
                        yield (2, 4)[c]
                        for b, off, name in (((1, 3)[c], 0, "f_g"), ((2, 0)[c], I0, "f_u")):
                            for k in range(KT):
                                w = slice(off + CH * c, off + CH * (c + 1))
                                last = product(B_[b][:, :], at_hi[:, k, :], at_lo[:, k, :],
                                               up_hi[:, k, w], up_lo[:, k, w], k == 0, k == KT - 1)
                            last.then_inc(S[f"{name}{c}"], 1)
                    for c, b in ((0, 1), (1, 3)):
                        yield (7, 10)[c]
                        wait(pe, f"f_hm{c}", i)
                        turn(B_[b], lambda k: hid[:, CH * c + P * k:CH * c + P * (k + 1)], 4).then_inc(S[f"f_t{c}"], 1)
                    for c in range(2):
                        yield (10, 13)[c]
                        wait(pe, f"f_th{c}", n)
                        wait(pe, f"f_tl{c}", n)
                        last = down(range(4 * c, 4 * c + 4), down_hi, down_lo, B_[2])
                    last.then_inc(S["f_y"], 1)
                else:
                    o = B_[1]
                    c0 = 2 * E * EI
                    for k in range(KT):
                        w = w13_r[:, k, c0:c0 + 2 * EI]
                        pe.matmul(o[:, 0:2 * EI], at_hi[:, k, :], w, start=(k == 0), stop=False, skip_group_check=True)
                        pe.matmul(o[:, 0:2 * EI], at_lo[:, k, :], w, start=False, stop=(k == KT - 1),
                                  skip_group_check=True)
                    for k in range(KT):
                        last = product(o[:, 2 * EI:SH], at_hi[:, k, :], at_lo[:, k, :], gate_hi[:, k, :],
                                       gate_lo[:, k, :], False, k == KT - 1, free=True)
                    last.then_inc(S["f_sh"], 1)
                    for q in range(4):
                        yield (3, 4, 6, 7)[q]
                        if q == 1:
                            wait(pe, "f_hs", i)
                        if q >= 2:
                            wait(pe, f"f_h{q - 2}", n)
                        for b, off, name in (((2, 0)[q % 2], 0, "f_g"), ((3, 1)[q % 2], PAIR, "f_u")):
                            for k in range(KT):
                                w = w13_r[:, k, 2 * PAIR * q + off:2 * PAIR * q + off + PAIR]
                                last = product(B_[b][:, 0:PAIR], at_hi[:, k, :], at_lo[:, k, :], w, None,
                                               k == 0, k == KT - 1)
                            last.then_inc(S[f"{name}{q}"], 1)
                    for t, b, q in ((0, 2, 2), (1, 3, 2), (2, 0, 3), (3, 1, 3)):
                        yield (8, 9)[t // 2]
                        wait(pe, f"f_h{q}", i)
                        turn(B_[b], lambda k: hid[:, CH * t + P * k:CH * t + P * (k + 1)], 4 if t < 3 else 1)\
                            .then_inc(S[f"f_t{t}"], 1)
                    for t in range(4):
                        yield 11 + t
                        wait(pe, f"f_th{t}", i if t > 1 else n)
                        wait(pe, f"f_tl{t}", i if t > 1 else n)
                        last = down(range(4 * t, 4 * t + (4 if t < 3 else 1)), w2_r, None, B_[2])
                    last.then_inc(S["f_y"], 1)

            rounds(pe, attention, ffn)

        @block.vector
        def _(dve):
            kh, kl = up_lo[0:C, 0, 0:B * T], up_lo[0:C, 1, 0:B * T]
            kt_raw = work[0:C, 0:B * T]
            dve.wait_ge(S["c_kh"], 1)
            dve.tensor_tensor(kl, kt_raw, kh.bitcast(F32), ALU.subtract).then_inc(S["c_kl"], 1)
            for s in range(2):
                dve.memset(k0a[s][:, :, :].bitcast(F32), 0.0).then_inc(S["c_oh"], 1)
            dve.wait_ge(S["c_sel"], 3)
            for s in range(2):
                one_hot = [pt[:, h, :].rearrange("p (g t) -> p g t", g=4) for h in (0, 2)]
                dve.tensor_copy(k0b[s][:, :, :], one_hot[0]).then_inc(S["c_oh"], 1)
                for t in range(2):
                    last = dve.tensor_copy(k1[s][:, 4 * t:4 * t + 4, :], one_hot[1])
                last.then_inc(S["c_oh"], 1)
            dve.wait_ge(S["c_tg"], 1)
            dve.tensor_scalar(bcg[:, :], bcg[:, :], tg[:, 0:1], None, ALU.mult).then_inc(S["c_vec"], 1)
            dve.wait_ge(S["c_hi"], 2)
            dve.tensor_tensor(gate_lo[:, :, :], gate_raw[:, :, :], gate_hi[:, :, :].bitcast(F32), ALU.subtract)\
               .then_inc(S["c_lo"], 1)
            dve.tensor_tensor(wc_lo[:, :, :], work[:, 2048:2048 + 2 * D].rearrange("p (k n) -> p k n", k=KT),
                              wc_hi[:, :, :].bitcast(F32), ALU.subtract).then_inc(S["c_lo"], 1)

            def split_ffn_0_weights():
                for k in range(KT):
                    dve.wait_ge(S["c_hi"], 3 + k)
                    dve.tensor_tensor(up_lo[:, k, :], work[:, 2048 * k:2048 * (k + 1)], up_hi[:, k, :].bitcast(F32),
                                      ALU.subtract).then_inc(S["c_lo"], 1)
                dve.wait_ge(S["c_hi"], 5)
                dve.tensor_tensor(down_lo[:, :, :], work[:, 0:(I0 // P) * D].rearrange("p (k n) -> p k n", n=D),
                                  down_hi[:, :, :].bitcast(F32), ALU.subtract).then_inc(S["c_lo"], 1)
                dve.wait_ge(S["c_lo"], 5)
                dve.memset(hid[:, I1:HW], 0.0).then_inc(S["c_vec"], 1)

            def norm(pre, n, src, stat, mv, rs, xn):
                dve.bn_stats(stat[:, :], src[:, :]).then_inc(S[pre + "stats"], 1)
                wait_alone(dve, pre + "stats", n)
                dve.bn_aggr(mv[:, :], stat[:, :]).then_inc(S[pre + "mvd"], 1)

            def norm_apply(pre, n, src, mv, rs, xn):
                wait(dve, pre + "rstd", n)
                dve.tensor_scalar(xn[:, :], src[:, :], mv[:, 0:1], rs[:, :], ALU.subtract, ALU.mult)\
                   .then_inc(S[pre + "norm"], 1)

            def attention(p, s, L):
                yield 0
                n, i = 4 * p + s + 2 * L, 2 * p + s
                B_ = bank[s]
                d = HD[L]
                src = x0[s] if L == 0 else x2[s]
                if L == 0:
                    dve.wait_ge(ld_x[s], 16 * (p + 1))
                else:
                    wait(dve, "f_out", n - 2)
                norm("a_", n, src, a_stat, a_mv, a_rs, a_xn)
                yield 1
                wait_before(dve, "a_q_lo", n)
                wait_before(dve, "a_q_hi2", n)
                norm_apply("a_", n, src, a_mv, a_rs, a_xn)
                step = 8 // G[L]
                order = [(j, t) for t in range(G[L] // 4) for j in range(HPG)]
                for m, (j, t) in enumerate(order):
                    yield 3 + m // 2
                    wait_part(dve, "a_m", n, step * (m + 1))
                    if L == 0:
                        o = q0b[:, j, :, HD0:HD0 + 1].rearrange("p g o -> p (g o)")
                    else:
                        o = q1[:, j, 4 * t:4 * t + 4, 3 * HD1:3 * HD1 + 1].rearrange("p g o -> p (g o)")
                    b = (1 + m) % 4 if L == 0 else (2 + m) % 4
                    dve.tensor_reduce(o, B_[b][:, :].rearrange("p (g t) -> p g t", t=T), AX.X, ALU.max, negate=True)\
                       .then_inc(S["a_r"], step)
                yield 13
                for t in range(G[L] // 4):
                    wait(dve, "a_otT" if t == 0 else "a_otT2", n if t == 0 else i)
                    o = (B_[3] if L == 0 else B_[t])[:, :].rearrange("p (j g b) -> p j g b", j=HPG, g=4)
                    r = rec[:, :, 4 * t:4 * t + 4]
                    dve.reciprocal(r, o[:, :, :, d:d + 1].rearrange("p j g o -> p j (g o)"))\
                       .then_inc(S["a_rec" if t == 0 else "a_rec2"], 1)
                    wait(dve, "a_rec" if t == 0 else "a_rec2", n if t == 0 else i)
                    ov = on[:, :].rearrange("p (g j d) -> p j g d", g=G[L], j=HPG)[:, :, 4 * t:4 * t + 4, :]
                    dve.tensor_tensor(ov, o[:, :, :, 0:d], r.unsqueeze(3).broadcast_to([P, HPG, 4, d]), ALU.mult)\
                       .then_inc(S["a_on" if t == 0 else "a_on2"], 1)
                if L == 0:
                    yield 14
                    wait(dve, "a_aohi", i)
                    dve.tensor_tensor(ao_lo[:, :, :], B_[0][:, 0:D].rearrange("p (k t) -> p k t", k=KT),
                                      ao_hi[:, :, :].bitcast(F32), ALU.subtract).then_inc(S["a_aolo"], 1)
                    yield 15
                    wait(dve, "a_proj", i)
                    wait(dve, "xb_done", i)
                    dve.scalar_tensor_tensor(out=x1[s][:, :], in0=B_[1][:, 0:D], scalar=tg[:, 0:1], in1=xb[s][:, :],
                                             op0=ALU.mult, op1=ALU.add).then_inc(S["a_out"], 1)
                else:
                    wait(dve, "a_on2", i)
                    dve.scalar_tensor_tensor(out=x3[s][:, :], in0=on[:, :], scalar=tg[:, 1:2], in1=x2[s][:, :],
                                             op0=ALU.mult, op1=ALU.add).then_inc(S["a_out"], 1)

            def ffn(p, s, L):
                yield 0
                n, i = 4 * p + s + 2 * L, 2 * p + s
                B_ = bank[s]
                src = x1[s] if L == 0 else x3[s]
                wait(dve, "a_out", n)
                norm("f_", n, src, f_stat, f_mv, f_rs, f_xn)
                yield 1
                norm_apply("f_", n, src, f_mv, f_rs, f_xn)
                wait(dve, "f_at_hi", n)
                dve.tensor_tensor(at_lo[:, :, :], B_[0][:, 0:D].rearrange("p (k t) -> p k t", k=KT),
                                  at_hi[:, :, :].bitcast(F32), ALU.subtract).then_inc(S["f_at_lo"], 1)

                def hidden_t(t, b, cols):
                    wait(dve, f"f_th{t}", i if t > 1 else n)
                    r = slice(4 * t, 4 * t + cols // P)
                    dve.tensor_tensor(ht_lo[:, r, :], B_[b][:, 0:cols].rearrange("p (k t) -> p k t", t=P),
                                      ht_hi[:, r, :].bitcast(F32), ALU.subtract).then_inc(S[f"f_tl{t}"], 1)

                if L == 0:
                    for c in range(2):
                        yield (3, 6)[c]
                        cols = slice(CH * c, CH * (c + 1))
                        wait(dve, f"f_sg{c}", n)
                        wait(dve, f"f_u{c}", n)
                        dve.tensor_tensor(hid[:, cols], B_[(2, 0)[c]][:, :], sg[:, cols], ALU.mult)\
                           .then_inc(S[f"f_h{c}"], 1)
                        yield (5, 8)[c]
                        wait(dve, f"f_abs{c}", i)
                        a = sg[:, cols].rearrange("p (n a e) -> p n a e", a=2, e=2)
                        dve.tensor_tensor(pmax[:, :, :], a[:, :, :, 0], a[:, :, :, 1], ALU.max)
                        dve.tensor_tensor(pmin[:, :, :], a[:, :, :, 0], a[:, :, :, 1], ALU.min)
                        dve.tensor_tensor(lose[:, :, :, 0], a[:, :, :, 0], a[:, :, :, 1], ALU.is_lt)
                        dve.tensor_tensor(lose[:, :, :, 1], a[:, :, :, 0], a[:, :, :, 1], ALU.is_ge)\
                           .then_inc(S["f_pairs"], 1)
                        dve.wait_ge(S["f_pairs"], 2 * i + 1 + c)
                        dve.tensor_tensor(both[:, 0, :], pmin[:, :, 0], pmax[:, :, 1], ALU.is_ge)
                        dve.tensor_tensor(both[:, 1, :], pmin[:, :, 1], pmax[:, :, 0], ALU.is_gt)\
                           .then_inc(S["f_cmp"], 1)
                        dve.wait_ge(S["f_cmp"], 2 * i + 1 + c)
                        dve.tensor_tensor(lead[:, :, 0], both[:, 0, :], both[:, 1, :], ALU.subtract)
                        dve.tensor_tensor(lead[:, :, 1], both[:, 1, :], both[:, 0, :], ALU.subtract)\
                           .then_inc(S["f_lead"], 1)
                        dve.wait_ge(S["f_lead"], 2 * i + 1 + c)
                        dve.tensor_tensor(keep[:, c, :].rearrange("p (n a e) -> p n a e", a=2, e=2),
                                          lead[:, :, :].unsqueeze(3).broadcast_to([P, NG, 2, 2]), lose[:, :, :, :],
                                          ALU.is_ge).then_inc(S[f"f_keep{c}"], 1)
                    for t, b in ((0, 1), (1, 3)):
                        yield (9, 12)[t]
                        hidden_t(t, b, 4 * P)
                    yield 14
                    wait(dve, "f_y", n)
                    dve.scalar_tensor_tensor(out=x2[s][:, :], in0=B_[2][:, 0:D], scalar=tg[:, 2:3], in1=x1[s][:, :],
                                             op0=ALU.mult, op1=ALU.add).then_inc(S["f_out"], 1)
                else:
                    yield 2
                    wait(dve, "f_sh", i)
                    dve.tensor_copy(lg[:, :], B_[1][:, 2 * EI:SH]).then_inc(S["f_lg"], 1)
                    wait(dve, "f_lg", i)
                    dve.scalar_tensor_tensor(out=rt[:, 0, :], in0=lg[:, :], scalar=-1.0, in1=lg[:, :],
                                             op0=ALU.mult, op1=ALU.min).then_inc(S["f_r1"], 1)
                    yield 3
                    wait(dve, "f_r2", i)
                    dve.tensor_scalar(rt[:, 2, :], rt[:, 1, :], 1.0, None, ALU.add).then_inc(S["f_r3"], 1)
                    wait(dve, "f_r3", i)
                    dve.tensor_scalar(rt[:, 4, :], rt[:, 2, :], -1.0, 2.0 ** -23, ALU.add, ALU.max).then_inc(S["f_r0"], 1)
                    wait(dve, "f_r0", i)
                    dve.reciprocal(rt[:, 5, :], rt[:, 4, :])
                    dve.tensor_scalar(rt[:, 6, :], rt[:, 1, :], -0.5, 1.0, ALU.mult, ALU.add).then_inc(S["f_r5"], 1)
                    wait(dve, "f_r5", i)
                    dve.tensor_tensor(rt[:, 5, :], rt[:, 5, :], rt[:, 1, :], ALU.mult)
                    dve.tensor_tensor(rt[:, 6, :], rt[:, 6, :], rt[:, 1, :], ALU.mult).then_inc(S["f_r6"], 1)
                    yield 4
                    wait(dve, "f_r4", i)
                    wait(dve, "f_r6", i)
                    dve.tensor_tensor(rt[:, 5, :], rt[:, 5, :], rt[:, 3, :], ALU.mult).then_inc(S["f_r9"], 1)
                    wait(dve, "f_r9", i)
                    dve.tensor_tensor(rt[:, 6, :], rt[:, 6, :], rt[:, 5, :], ALU.max).then_inc(S["f_r10"], 1)
                    wait(dve, "f_r10", i)
                    dve.scalar_tensor_tensor(out=rt[:, 7, :], in0=lg[:, :], scalar=0.0, in1=rt[:, 6, :],
                                             op0=ALU.max, op1=ALU.add).then_inc(S["f_r7"], 1)
                    wait(dve, "f_sgs", i)
                    dve.tensor_tensor(hid[:, E * EI:I1], B_[1][:, EI:2 * EI], sg[:, E * EI:I1], ALU.mult)\
                       .then_inc(S["f_hs"], 1)
                    yield 5
                    wait(dve, "f_r8", i)
                    dve.tensor_tensor(rt[:, 9, :], rt[:, 8, :], gb[:, :], ALU.add).then_inc(S["f_r11"], 1)
                    wait(dve, "f_r11", i)
                    own = rt[:, 9, :].unsqueeze(2).broadcast_to([P, E, E])
                    other = rt[:, 9, :].unsqueeze(1).broadcast_to([P, E, E])
                    dve.tensor_tensor(cmp[:, 0], other, own, ALU.is_ge)
                    dve.tensor_tensor(cmp[:, 1], other, own, ALU.is_gt).then_inc(S["f_cmp2"], 1)
                    wait(dve, "f_cmp2", i)
                    dve.tensor_tensor(cmp[:, :, :, :], cmp[:, :, :, :], tie[:, :, :, :], ALU.mult)\
                       .then_inc(S["f_cmp3"], 1)
                    wait(dve, "f_cmp3", i)
                    dve.tensor_reduce(rank[:, :], cmp[:, :, :, :].rearrange("p a e f -> p e a f"), AX.XY, ALU.add)\
                       .then_inc(S["f_rank"], 1)
                    wait(dve, "f_rank", i)
                    dve.scalar_tensor_tensor(out=cw[:, :], in0=rank[:, :], scalar=1.5, in1=rt[:, 8, :],
                                             op0=ALU.is_lt, op1=ALU.mult).then_inc(S["f_cw"], 1)
                    wait(dve, "f_cw", i)
                    for q in range(4):
                        yield 6 + q
                        wait(dve, f"f_sg{q}", n if q < 2 else i)
                        wait(dve, f"f_u{q}", n if q < 2 else i)
                        for k in range(2):
                            e = 2 * q + k
                            last = dve.scalar_tensor_tensor(
                                out=hid[:, EI * e:EI * (e + 1)], in0=B_[(3, 1)[q % 2]][:, EI * k:EI * (k + 1)],
                                scalar=cw[:, e:e + 1], in1=sg[:, EI * e:EI * (e + 1)], op0=ALU.mult, op1=ALU.mult)
                        last.then_inc(S[f"f_h{q}"], 1)
                    for t, b in ((0, 2), (1, 3), (2, 0), (3, 1)):
                        yield 10 + t
                        hidden_t(t, b, 4 * P if t < 3 else P)
                    yield 14
                    wait(dve, "f_y", n)
                    if not (isinstance(p, int) and p == 0):
                        dve.wait_ge(st_y[s], 16 * p)
                    dve.scalar_tensor_tensor(out=y[s][:, :], in0=B_[2][:, 0:D], scalar=tg[:, 3:4], in1=x3[s][:, :],
                                             op0=ALU.mult, op1=ALU.add).then_inc(S["f_out"], 1)

            rounds(dve, attention, ffn, split_ffn_0_weights)


_IN = ["x", "ctx_kv", "ctx_t", "g_x", "g_f", "wc_t", "bc", "w_up", "w_down", "gate_w_t", "gate_b", "w13", "w2"]


def kernel(x, ctx_512, g_xattn, g_ffn, L0_xattn_Wc, L0_xattn_bc, L0_ffn_w_gate, L0_ffn_w_up, L0_ffn_w_down,
           L1_ffn_gate_w, L1_ffn_gate_b, L1_ffn_w1, L1_ffn_w2, L1_ffn_w3, L1_ffn_sw1, L1_ffn_sw2, L1_ffn_sw3):
    import concourse.bacc as bacc
    from concourse.bass_utils import run_bass_kernel_spmd

    E, EI, D = L1_ffn_w1.shape
    up = []
    for q in range(E // 2):
        up += [L1_ffn_w1[2 * q], L1_ffn_w1[2 * q + 1], L1_ffn_w3[2 * q], L1_ffn_w3[2 * q + 1]]
    w13 = np.concatenate(up + [L1_ffn_sw1, L1_ffn_sw3], axis=0).T
    w2 = np.concatenate([L1_ffn_w2.transpose(0, 2, 1).reshape(E * EI, D), np.asarray(L1_ffn_sw2).T], axis=0)
    arrays = {
        "x": x, "ctx_kv": ctx_512, "ctx_t": ctx_512.transpose(2, 0, 1).reshape(ctx_512.shape[2], -1),
        "g_x": g_xattn, "g_f": g_ffn, "wc_t": L0_xattn_Wc.T, "bc": L0_xattn_bc,
        "w_up": np.concatenate([L0_ffn_w_gate, L0_ffn_w_up], axis=1), "w_down": L0_ffn_w_down,
        "gate_w_t": L1_ffn_gate_w.T, "gate_b": L1_ffn_gate_b, "w13": w13, "w2": w2,
    }
    arrays = {f"in_{k}": np.ascontiguousarray(v) for k, v in arrays.items()}
    nc = bacc.Bacc("TRN2", target_bir_lowering=False, num_devices=1)
    args = [nc.dram_tensor(f"in_{k}", arrays[f"in_{k}"].shape, mybir.dt.from_np(arrays[f"in_{k}"].dtype),
                           kind="ExternalInput").ap() for k in _IN]
    out = nc.dram_tensor("out", arrays["in_x"].shape, F32, kind="ExternalOutput").ap()
    flamingo_block(nc, *args, out)
    return run_bass_kernel_spmd(nc, [arrays], core_ids=[0]).results[0]["out"]
```

```python
from contextlib import ExitStack

import numpy as np

import concourse.bass as bass
from concourse import mybir

ALU = mybir.AluOpType
ACT = mybir.ActivationFunctionType
F32 = mybir.dt.float32
F32R = mybir.dt.float32r
BF16 = mybir.dt.bfloat16
AX = mybir.AxisListType



def flamingo_block(nc, x, ctx_kv, ctx_t, g_x, g_f, wc_t, bc, w_up, w_down, gate_w_t, gate_b, w13, w2, out):
    B, T, D = x.shape
    C = ctx_kv.shape[2]
    P = 128
    assert T == P and D == 2 * P and C == 64
    KT = D // P
    G0, HD0 = 4, 16
    G1, HD1 = 8, 8
    HPG = 4
    BLK = 32
    I0 = w_down.shape[0]
    E = gate_b.shape[0]
    EI = 176
    I1 = (E + 1) * EI
    NT1 = -(-I1 // P)
    PAIR = 2 * EI
    SH = 2 * EI + E
    EPS = 1e-5
    NS = 4
    RND = B // NS
    assert I0 == 8 * P and E == 8

    ctx = ExitStack()
    with ctx:
        def sb(name, shape, dt=F32):
            return ctx.enter_context(nc.sbuf_tensor(name, shape, dt))

        def sem(name):
            return ctx.enter_context(nc.semaphore(name))

        up_hi = sb("up_hi", [P, KT, 2 * I0], F32R)
        up_lo = sb("up_lo", [P, KT, 2 * I0], F32R)
        down_hi = sb("down_hi", [P, I0 // P, D], F32R)
        down_lo = sb("down_lo", [P, I0 // P, D], F32R)
        wc_hi = sb("wc_hi", [P, KT, D], F32R)
        wc_lo = sb("wc_lo", [P, KT, D], F32R)
        w13_r = sb("w13_r", [P, KT, 2 * I1], F32R)
        gate_hi = sb("gate_hi", [P, KT, E], F32R)
        gate_lo = sb("gate_lo", [P, KT, E], F32R)
        w2_r = sb("w2_r", [P, NT1, D], F32R)
        gate_raw = sb("gate_raw", [P, KT, E])
        gb = sb("gb", [P, E])
        bcg = sb("bcg", [P, D])
        graw = sb("graw", [P, 4])
        tg = sb("tg", [P, 4])
        ident = sb("ident", [P, P])
        neg_half = sb("neg_half", [P, 1])
        half = sb("half", [P, E])
        tie = sb("tie", [P, 2, E, E], BF16)

        xr = [sb(f"xr_{s}", [P, D]) for s in range(NS)]
        v1 = [sb(f"v1_{s}", [P, G1, BLK]) for s in range(NS)]

        x0 = [sb(f"x0_{b}", [P, D]) for b in range(2)]
        y = [sb(f"y_{b}", [P, D]) for b in range(2)]
        ct = [sb(f"ct_{b}", [P, C]) for b in range(2)]
        v0 = [sb(f"v0_{b}", [P, G0, BLK]) for b in range(2)]
        k0a = [sb(f"k0a_{s}", [P, G0, T], F32R) for s in range(2)]
        k0b = [sb(f"k0b_{s}", [P, G0, T], F32R) for s in range(2)]
        k1 = [sb(f"k1_{s}", [P, G1, T], F32R) for s in range(2)]

        a_stat = sb("a_stat", [P, 6])
        a_mv = sb("a_mv", [P, 2])
        a_ve = sb("a_ve", [P, 1])
        a_rs = sb("a_rs", [P, 1])
        a_xn = sb("a_xn", [P, D])
        q0a = sb("q0a", [P, HPG, G0, BLK])
        q0b = sb("q0b", [P, HPG, G0, BLK])
        q1 = sb("q1", [P, HPG, G1, BLK])
        qt = [sb(f"qt{b}", [P, 2, HPG * T], F32R) for b in range(2)]
        pt = sb("pt", [P, G1, HPG * T])
        ot = sb("ot", [P, 2, HPG * T])
        rec = sb("rec", [P, HPG, G1])
        on = sb("on", [P, D])
        ao_hi = sb("ao_hi", [P, KT, P], F32R)
        ao_lo = sb("ao_lo", [P, KT, P], F32R)

        f_stat = sb("f_stat", [P, 6])
        f_mv = sb("f_mv", [P, 2])
        f_ve = sb("f_ve", [P, 1])
        f_rs = sb("f_rs", [P, 1])
        f_xn = sb("f_xn", [P, D])
        at_hi = [sb(f"at_hi{b}", [P, KT, P], F32R) for b in range(2)]
        at_lo = [sb(f"at_lo{b}", [P, KT, P], F32R) for b in range(2)]
        HW = NT1 * P
        work = sb("work", [P, 2 * HW + 2 * I0])
        hid = [work[:, HW * b:HW * (b + 1)] for b in range(2)]
        sg = [work[:, 2 * HW + I0 * b:2 * HW + I0 * (b + 1)] for b in range(2)]
        ht_hi = sb("ht_hi", [P, NT1, P], F32R)
        ht_lo = sb("ht_lo", [P, NT1, P], F32R)
        CH = 512
        NG = CH // 4
        pmax = sb("pmax", [P, NG, 2])
        pmin = sb("pmin", [P, NG, 2])
        lose = sb("lose", [P, NG, 2, 2], BF16)
        both = sb("both", [P, 2, NG], BF16)
        lead = sb("lead", [P, NG, 2], BF16)
        keep = sb("keep", [P, 2, CH], BF16)
        lg = sb("lg", [P, E])
        rt = sb("rt", [P, 10, E])
        cmp = sb("cmp", [P, 2, E, E], BF16)
        rank = sb("rank", [P, E])
        cw = [sb(f"cw{b}", [P, E]) for b in range(2)]

        half_bank = [[ctx.enter_context(nc.psum_tensor(f"bank{h}{b}", [P, 512], F32)) for b in range(2)]
                     for h in range(4)]
        QK, PV, UP, DOWN = half_bank

        kd0a = nc.dram_tensor("kd0a", (G0, 2, HD0, B * T), F32, kind="Internal").ap()
        kd0b = nc.dram_tensor("kd0b", (G0, HD0, B * T), F32, kind="Internal").ap()
        kd1 = nc.dram_tensor("kd1", (G1, 3, HD1, B * T), F32, kind="Internal").ap()

        names = """
        ld_kt ld_small ld_up ld_down ld_wc ld_w13 ld_w2 scratch_kd
        c_mem c_sel c_oh c_tg c_hi c_kh c_kl c_lo c_vec
        xb_done v0_done v1_done
        a_stats a_mvd a_veps a_rstd a_norm a_q_hi a_q_hi2 a_q_lo a_qt_ps a_qt_ps2 a_qt a_qt2
        a_m a_r a_mt_ps a_mt_ps2 a_mt a_mt2 a_mclear a_s a_e
        a_pv a_pv2 a_ot a_ot2 a_otT a_otT2 a_rec a_rec2 a_on a_on2 a_onT a_aohi a_aolo a_proj a_out
        f_stats f_mvd f_veps f_rstd f_norm f_xt_ps f_at_hi f_at_lo
        f_g0 f_u0 f_g1 f_u1 f_sg0 f_sg1 f_h0 f_h1 f_g2 f_u2 f_g3 f_u3 f_sg2 f_sg3 f_h2 f_h3
        f_abs0 f_abs1 f_pairs f_cmp f_lead f_cmp2 f_cmp3 f_rank f_keep0 f_keep1 f_hm0 f_hm1
        f_sh f_ro f_lg f_sgs f_hs f_r0 f_r1 f_r2 f_r3 f_r4 f_r5 f_r6 f_r7 f_r8 f_r9 f_r10 f_r11 f_cw
        f_t0 f_t1 f_t2 f_t3 f_th0 f_th1 f_th2 f_th3 f_tl0 f_tl1 f_tl2 f_tl3 f_y f_out
        """.split()
        S = {n: sem(n) for n in names}
        ld_x = [sem(f"ld_x{b}") for b in range(2)]
        ld_ct = [sem(f"ld_ct{b}") for b in range(2)]
        ld_k0 = [sem(f"ld_k0{s}") for s in range(2)]
        ld_k1 = [sem(f"ld_k1{s}") for s in range(2)]
        st_y = [sem(f"st_y{b}") for b in range(2)]

        def wait(eng, name, n):
            eng.wait_ge(S[name], n + 1)

        def wait_before(eng, name, n, back=1):
            if not (isinstance(n, int) and n < back):
                eng.wait_ge(S[name], n + 1 - back)

        def wait_part(eng, name, n, k):
            eng.wait_ge(S[name], 8 * n + k)

        def wait_alone(eng, name, n, back=0):
            if isinstance(n, int) and n < back:
                return
            count = n + 1 - back
            if not isinstance(count, int):
                count = eng.snap(eng.to_reg(count))
            eng.wait_ge(S["c_mem"], 15)
            eng.wait_ge(S[name], count)

        STEPS = 8

        def alternate(*halves):
            at = {h: next(h) for h in halves}
            for step in range(STEPS):
                for h in halves:
                    while at[h] is not None and at[h] <= step:
                        at[h] = next(h, None)

        def rounds(eng, halves, weights=None):
            def slot(p, t, first=0):
                now = []
                for h in range(first, 4):
                    q, k = (p, t - h) if t >= h else (p - 1, t - h + 2 * NS)
                    if not (isinstance(q, int) and q < 0):
                        now.append(halves[h](q, k % NS, k // NS))
                alternate(*[now[k] for k in ORDER if k < len(now)])

            def body(p):
                for t in range(2 * NS):
                    slot(p, t)
                    if weights and isinstance(p, int) and t == 1:
                        weights()

            body(0)
            with eng.Fori(1, RND) as p:
                body(p)
            for t in range(3):
                slot(RND, t, first=t + 1)

        ORDER = (1, 3, 0, 2)

        def use(p, s):
            return NS // 2 * p + s // 2 + 1

        def halves_index(p, s, L):
            return 2 * NS * p + NS * L + s, NS * p + s, s % 2

        block = ctx.enter_context(nc.Block())
        G = [G0, G1]
        HD = [HD0, HD1]

        @block.sync
        def _(sp):
            kt_raw = work[0:C, 0:B * T]
            sp.dma_start(kt_raw, ctx_t).then_inc(S["ld_kt"], 16)
            sp.dma_start(graw[:, 0:2], g_x.partition_broadcast(P)).then_inc(S["ld_small"], 16)
            sp.dma_start(graw[:, 2:4], g_f.partition_broadcast(P)).then_inc(S["ld_small"], 16)
            sp.dma_start(bcg[:, :], bc.partition_broadcast(P)).then_inc(S["ld_small"], 16)
            sp.dma_start(gb[:, :], gate_b.partition_broadcast(P)).then_inc(S["ld_small"], 16)
            sp.dma_start(gate_raw[:, :, :], gate_w_t.rearrange("(k p) e -> p k e", p=P)).then_inc(S["ld_small"], 16)

            def load_x(i, s):
                sp.dma_start(x0[s][:, :], x[i]).then_inc(ld_x[s], 16)
                sp.dma_start(ct[s][:, :], ctx_kv[i]).then_inc(ld_ct[s], 16)

            def load_k0(i, s):
                for g in range(G0):
                    sp.dma_start(k0a[s][BLK * g:BLK * (g + 1), g, :].bitcast(F32),
                                 kd0a[g].rearrange("a d (b t) -> (a d) b t", t=T)[:, i, :]).then_inc(ld_k0[s], 16)
                    sp.dma_start(k0b[s][BLK * g:BLK * g + HD0, g, :].bitcast(F32),
                                 kd0b[g].rearrange("d (b t) -> d b t", t=T)[:, i, :]).then_inc(ld_k0[s], 16)

            def load_k1(i, s):
                for g in range(G1):
                    r = BLK * (g % 4)
                    sp.dma_start(k1[s][r:r + 3 * HD1, g, :].bitcast(F32),
                                 kd1[g].rearrange("a d (b t) -> (a d) b t", t=T)[:, i, :]).then_inc(ld_k1[s], 16)

            for s in range(2):
                load_x(s, s)
            sp.wait_ge(S["scratch_kd"], 16 * (2 * G0 + 1 + 3 * G1))
            sp.wait_ge(S["c_oh"], 3 * 2)
            for s in range(2):
                load_k0(s, s)
            for s in range(2):
                load_k1(s, s)

            def store(p, s):
                wait(sp, "f_out", 2 * NS * p + NS + s)
                sp.dma_start(out[NS * p + s], y[s % 2][:, :]).then_inc(st_y[s % 2], 16)

            def body(p, last=False):
                for s in range(NS):
                    n, i, b = halves_index(p, s, 0)
                    if not (isinstance(p, int) and p == 0):
                        store(p - 1, s)
                    if not (last and s >= 2):
                        wait(sp, "a_norm", n)
                        wait(sp, "xb_done", i)
                        wait(sp, "v0_done", i)
                        wait(sp, "v1_done", i)
                        load_x(i + 2, b)
                    if not (last and s >= 2):
                        wait_part(sp, "a_s", n, 8)
                        load_k0(i + 2, b)
                for s in range(NS):
                    n, i, b = halves_index(p, s, 1)
                    if not (last and s >= 2):
                        wait_part(sp, "a_s", n, 8)
                        load_k1(i + 2, b)

            body(0)
            with sp.Fori(1, RND - 1) as p:
                body(p)
            body(RND - 1, last=True)
            for s in range(NS):
                store(RND - 1, s)
            for b in range(2):
                sp.wait_ge(st_y[b], 16 * RND * NS // 2)

        @block.gpsimd
        def _(pool):
            for t in (q0a, q0b, q1):
                pool.memset(t[:, :, :, :], 0.0).then_inc(S["c_mem"], 1)
            for t in (pt[:, 0:4, :], w2_r[:, NT1 - 1, :].bitcast(F32)):
                pool.memset(t, 0.0).then_inc(S["c_mem"], 1)
            for t in (*v0, *v1):
                pool.memset(t[:, :, :], 0.0).then_inc(S["c_mem"], 1)
            pool.memset(ident[:, :], 0.0).then_inc(S["c_mem"], 1)
            pool.memset(neg_half[:, :], -0.5).then_inc(S["c_mem"], 1)
            pool.memset(half[:, :], 0.5).then_inc(S["c_mem"], 1)
            pool.memset(tie[:, :, :, :], 0.0).then_inc(S["c_mem"], 1)
            pool.wait_ge(S["c_mem"], 15)
            pool.dma_start(w13_r[:, :, :], w13.rearrange("(k p) n -> p k n", p=P)).then_inc(S["ld_w13"], 16)
            full = (NT1 - 1) * P
            pool.dma_start(w2_r[:, 0:NT1 - 1, :], w2[0:full].rearrange("(k p) n -> p k n", p=P)).then_inc(S["ld_w2"], 16)
            pool.dma_start(w2_r[0:I1 - full, NT1 - 1, :], w2[full:I1]).then_inc(S["ld_w2"], 16)
            pool.affine_select(out=ident[:, :], in_=ident[:, :], compare_op=ALU.not_equal, fill=1.0,
                               base=0, pattern=[[-1, P]], channel_multiplier=1).then_inc(S["c_sel"], 1)
            for half_, row in ((0, HD0), (2, 3 * HD1)):
                v = pt[:, half_, :].rearrange("p (g t) -> p g t", g=4)
                pool.affine_select(out=v, in_=v, compare_op=ALU.not_equal, fill=1.0, base=-row,
                                   pattern=[[-BLK, 4], [0, T]], channel_multiplier=1).then_inc(S["c_sel"], 1)
            for t, d in (*((t, HD0) for t in v0), *((t, HD1) for t in v1)):
                pool.memset(t[:, :, d:d + 1], 1.0).then_inc(S["c_sel"], 1)
            pool.affine_select(out=tie[:, 0], in_=tie[:, 0], compare_op=ALU.is_ge, fill=1.0,
                               base=0, pattern=[[-1, E], [1, E]], channel_multiplier=0).then_inc(S["c_sel"], 1)
            pool.affine_select(out=tie[:, 1], in_=tie[:, 1], compare_op=ALU.is_ge, fill=1.0,
                               base=0, pattern=[[1, E], [-1, E]], channel_multiplier=0).then_inc(S["c_sel"], 1)
            pool.wait_ge(S["c_vec"], 1)

            def rstd(pre, n, mv, ve, rs):
                wait_alone(pool, pre + "mvd", n)
                pool.tensor_scalar(ve[:, :], mv[:, 1:2], EPS, None, ALU.add).then_inc(S[pre + "veps"], 1)
                wait(pool, pre + "veps", n)
                pool.tensor_tensor(rs[:, :], ve[:, :], neg_half[:, :], ALU.pow).then_inc(S[pre + "rstd"], 1)

            def attention_1(p, s, L):
                yield 0
                n, i, b = halves_index(p, s, L)
                rstd("a_", n, a_mv, a_ve, a_rs)
                yield 1
                wait(pool, "a_q_hi", n)
                d = HD[L]
                q = q0a if L == 0 else q1
                xv = a_xn[:, :].rearrange("p (g j d) -> p j g d", g=G[L], j=HPG)
                for j in range(HPG):
                    last = pool.tensor_tensor(q[:, j, :, d:2 * d], xv[:, j], q[:, j, :, 0:d], ALU.subtract)
                last.then_inc(S["a_q_lo"], 1)
                yield 2
                if L == 0:
                    pool.wait_ge(ld_x[b], 16 * use(p, s))
                    wait_before(pool, "f_out", n, NS)
                    pool.tensor_tensor(xr[s][:, :], x0[b][:, :], bcg[:, :], ALU.add).then_inc(S["xb_done"], 1)
                    wait_alone(pool, "a_pv", n, 2 if s >= 2 else 2 + NS)
                    pool.wait_ge(ld_ct[b], 16 * use(p, s))
                    pool.tensor_copy(v0[b][:, :, 0:HD0], ct[b][:, :].rearrange("p (g d) -> p g d", g=G0))\
                        .then_inc(S["v0_done"], 1)
                    wait_alone(pool, "a_pv2", i, NS)
                    pool.tensor_copy(v1[s][:, :, 0:HD1], ct[b][:, :].rearrange("p (g d) -> p g d", g=G1))\
                        .then_inc(S["v1_done"], 1)
                else:
                    yield 7
                    wait_alone(pool, "a_mt_ps2", i)
                    pool.memset(q1[:, :, :, 3 * HD1:3 * HD1 + 1], 0.0).then_inc(S["a_mclear"], 1)

            def attention_2(p, s, L):
                yield 0

            def ffn_1(p, s, L):
                yield 0
                n, i, b = halves_index(p, s, L)
                rstd("f_", n, f_mv, f_ve, f_rs)
                if L == 1:
                    yield 4
                    wait(pool, "f_r7", i)
                    pool.tensor_tensor(rt[:, 8, :], rt[:, 7, :], half[:, :], ALU.pow).then_inc(S["f_r8"], 1)

            def ffn_2(p, s, L):
                yield 0
                n, i, b = halves_index(p, s, L)
                if L == 0:
                    for c in range(2):
                        yield c
                        wait(pool, f"f_keep{c}", i)
                        h = hid[b][:, CH * c:CH * (c + 1)]
                        pool.tensor_tensor(h, h, keep[:, c, :], ALU.mult).then_inc(S[f"f_hm{c}"], 1)

            rounds(pool, (attention_1, attention_2, ffn_1, ffn_2))

        @block.scalar
        def _(act):
            kt_raw = work[0:C, 0:B * T]
            act.dma_start(work[:, 2048:2048 + 2 * D].rearrange("p (k n) -> p k n", k=KT),
                          wc_t.rearrange("(k p) n -> p k n", p=P)).then_inc(S["ld_wc"], 16)
            kh = ht_hi[0:C, :, :].rearrange("p a b -> p (a b)")
            act.wait_ge(S["ld_kt"], 16)
            kh = up_lo[0:C, 0, 0:B * T]
            act.activation(kh, kt_raw, ACT.Copy).then_inc(S["c_kh"], 1)
            act.wait_ge(S["ld_small"], 16 * 5)
            act.activation(tg[:, :], graw[:, :], ACT.Tanh).then_inc(S["c_tg"], 1)
            act.activation(gate_hi[:, :, :], gate_raw[:, :, :], ACT.Copy).then_inc(S["c_hi"], 1)
            act.wait_ge(S["ld_wc"], 16)
            act.activation(wc_hi[:, :, :], work[:, 2048:2048 + 2 * D].rearrange("p (k n) -> p k n", k=KT), ACT.Copy)\
               .then_inc(S["c_hi"], 1)
            act.wait_ge(S["c_kh"], 1)
            for g in range(G0):
                for a in range(2):
                    act.dma_start(kd0a[g, a], kh[HD0 * g:HD0 * (g + 1), :].bitcast(F32)).then_inc(S["scratch_kd"], 16)
            for g in range(G1):
                for a in range(2):
                    act.dma_start(kd1[g, a], kh[HD1 * g:HD1 * (g + 1), :].bitcast(F32)).then_inc(S["scratch_kd"], 16)
            kl = up_lo[0:C, 1, 0:B * T]
            act.wait_ge(S["c_kl"], 1)
            act.dma_start(kd0b.rearrange("g d n -> (g d) n"), kl.bitcast(F32)).then_inc(S["scratch_kd"], 16)
            for g in range(G1):
                act.dma_start(kd1[g, 2], kl[HD1 * g:HD1 * (g + 1), :].bitcast(F32)).then_inc(S["scratch_kd"], 16)
            act.wait_ge(S["scratch_kd"], 16 * (2 * G0 + 1 + 3 * G1))
            act.wait_ge(S["c_lo"], 2)
            st_up = [work[:, 0:2048], work[:, 2048:4096]]
            for k in range(KT):
                act.dma_start(st_up[k], w_up[k * P:(k + 1) * P, :]).then_inc(S["ld_up"], 16)

            def round_ffn_0_weights():
                act.wait_ge(S["ld_up"], 32)
                for k in range(KT):
                    act.activation(up_hi[:, k, :], st_up[k], ACT.Copy).then_inc(S["c_hi"], 1)
                act.wait_ge(S["c_lo"], 4)
                st_down = work[:, 0:(I0 // P) * D].rearrange("p (k n) -> p k n", n=D)
                act.dma_start(st_down, w_down.rearrange("(k p) n -> p k n", p=P)).then_inc(S["ld_down"], 16)
                act.wait_ge(S["ld_down"], 16)
                act.activation(down_hi[:, :, :], st_down, ACT.Copy).then_inc(S["c_hi"], 1)

            def attention_1(p, s, L):
                yield 1
                n, i, b = halves_index(p, s, L)
                d = HD[L]
                wait(act, "a_norm", n)
                xv = a_xn[:, :].rearrange("p (g j d) -> p j g d", g=G[L], j=HPG)
                if L == 0:
                    wait_before(act, "a_mt_ps", n)
                    act.activation(q0a[:, :, :, 0:d].bitcast(F32R), xv, ACT.Copy).then_inc(S["a_q_hi"], 1)
                    act.activation(q0b[:, :, :, 0:d].bitcast(F32R), xv, ACT.Copy).then_inc(S["a_q_hi2"], 1)
                else:
                    act.activation(q1[:, :, :, 0:d].bitcast(F32R), xv, ACT.Copy).then_inc(S["a_q_hi"], 1)
                    act.activation(q1[:, :, :, 2 * d:3 * d].bitcast(F32R), xv, ACT.Copy).then_inc(S["a_q_hi2"], 1)
                yield 2
                wait(act, "a_qt_ps", n)
                act.activation(qt[b][:, 0, :], QK[0][:, :], ACT.Copy).then_inc(S["a_qt"], 1)
                if L == 1:
                    wait(act, "a_qt_ps2", i)
                    act.activation(qt[b][:, 1, :], QK[1][:, :], ACT.Copy).then_inc(S["a_qt2"], 1)
                yield 7
                wait(act, "a_mt_ps", n)
                if L == 0:
                    act.activation(qt[b][:, 1, :], QK[1][:, :], ACT.Copy).then_inc(S["a_mt"], 1)
                else:
                    act.activation(qt[b][:, 0, :], QK[0][:, :], ACT.Copy).then_inc(S["a_mt"], 1)
                    wait(act, "a_mt_ps2", i)
                    act.activation(qt[b][:, 1, :], QK[1][:, :], ACT.Copy).then_inc(S["a_mt2"], 1)

            def attention_2(p, s, L):
                yield 0
                n, i, b = halves_index(p, s, L)
                step = 8 // G[L]
                for g in range(G[L]):
                    yield g // 2
                    wait_part(act, "a_s", n, step * (g + 1))
                    act.activation(pt[:, g, :], PV[g % 2][:, :], ACT.Exp, scale=float(HD[L]) ** -0.5)\
                       .then_inc(S["a_e"], step)
                yield 4
                wait(act, "a_pv", n)
                act.activation(ot[:, 0, :], PV[0][:, :], ACT.Copy).then_inc(S["a_ot"], 1)
                if L == 1:
                    wait(act, "a_pv2", i)
                    act.activation(ot[:, 1, :], PV[1][:, :], ACT.Copy).then_inc(S["a_ot2"], 1)
                yield 6
                if L == 0:
                    wait(act, "a_onT", i)
                    act.activation(ao_hi[:, :, :], PV[0][:, 0:D].rearrange("p (k t) -> p k t", k=KT), ACT.Copy)\
                       .then_inc(S["a_aohi"], 1)

            def ffn_1(p, s, L):
                yield 1
                n, i, b = halves_index(p, s, L)
                wait(act, "f_xt_ps", n)
                act.activation(at_hi[b][:, :, :], UP[0][:, 0:D].rearrange("p (k t) -> p k t", k=KT), ACT.Copy)\
                   .then_inc(S["f_at_hi"], 1)
                if L == 0:
                    for c in range(2):
                        yield (3, 5)[c]
                        wait(act, f"f_g{c}", n)
                        act.activation(sg[b][:, CH * c:CH * (c + 1)], UP[0][:, :], ACT.Silu)\
                           .then_inc(S[f"f_sg{c}"], 1)
                        yield (4, 6)[c]
                        wait(act, f"f_h{c}", n)
                        act.activation(sg[b][:, CH * c:CH * (c + 1)], hid[b][:, CH * c:CH * (c + 1)], ACT.Abs)\
                           .then_inc(S[f"f_abs{c}"], 1)
                else:
                    yield 3
                    wait(act, "f_r1", i)
                    act.activation(rt[:, 1, :], rt[:, 0, :], ACT.Exp).then_inc(S["f_r2"], 1)
                    yield 4
                    wait(act, "f_r3", i)
                    act.activation(rt[:, 3, :], rt[:, 2, :], ACT.Ln).then_inc(S["f_r4"], 1)
                    wait(act, "f_sh", i)
                    act.activation(sg[b][:, 2 * PAIR:2 * PAIR + EI], UP[0][:, 0:EI], ACT.Silu)\
                       .then_inc(S["f_sgs"], 1)
                    yield 6
                    wait(act, "f_g0", n)
                    act.activation(sg[b][:, 0:PAIR], UP[0][:, 0:PAIR], ACT.Silu).then_inc(S["f_sg0"], 1)

            def hidden_t(n, t, b, cols):
                wait(act, f"f_t{t}", n)
                act.activation(ht_hi[:, 4 * t:4 * t + cols // P, :],
                               DOWN[b][:, 0:cols].rearrange("p (k t) -> p k t", t=P), ACT.Copy)\
                   .then_inc(S[f"f_th{t}"], 1)

            def ffn_2(p, s, L):
                yield 0
                n, i, b = halves_index(p, s, L)
                if L == 0:
                    for t in range(2):
                        yield (2, 4)[t]
                        hidden_t(n, t, 0, 4 * P)
                else:
                    hidden_t(i, 3, 1, P)
                    for q in range(1, 4):
                        yield q
                        wait(act, f"f_g{q}", n if q < 2 else i)
                        r = PAIR * (q % 2)
                        act.activation(sg[b][:, r:r + PAIR], DOWN[0][:, 0:PAIR], ACT.Silu)\
                           .then_inc(S[f"f_sg{q}"], 1)
                    yield 4
                    for t in range(2):
                        hidden_t(n, t, t, 4 * P)
                    yield 5
                    hidden_t(i, 2, 0, 4 * P)

            rounds(act, (attention_1, attention_2, ffn_1, ffn_2), round_ffn_0_weights)

        @block.tensor
        def _(pe):
            pe.wait_ge(S["c_sel"], 11)
            pe.wait_ge(S["c_mem"], 15)

            def product(o, a_hi, a_lo, w_hi, w_lo, first, last, free=False):
                pe.matmul(o, a_hi, w_hi, start=first, stop=False, skip_group_check=free)
                if w_lo is not None:
                    pe.matmul(o, a_hi, w_lo, start=False, stop=False, skip_group_check=free)
                return pe.matmul(o, a_lo, w_hi, start=False, stop=last, skip_group_check=free)

            def turn(o, src, count):
                for k in range(count):
                    last = pe.transpose(o[:, P * k:P * (k + 1)], src(k), ident[:, :])
                return last

            def attention_1(p, s, L):
                yield 2
                n, i, b = halves_index(p, s, L)
                tiles = G[L] // 4
                step = 8 // G[L]
                if L == 1:
                    wait_before(pe, "a_mclear", i)
                wait(pe, "a_q_hi", n)
                wait(pe, "a_q_lo", n)
                if L == 0:
                    turn(QK[0], lambda j: q0a[:, j].rearrange("p g b -> p (g b)"), HPG).then_inc(S["a_qt_ps"], 1)
                else:
                    wait(pe, "a_q_hi2", n)
                    turn(QK[0], lambda j: q1[:, j, 0:4].rearrange("p g b -> p (g b)"), HPG).then_inc(S["a_qt_ps"], 1)
                    turn(QK[1], lambda j: q1[:, j, 4:8].rearrange("p g b -> p (g b)"), HPG).then_inc(S["a_qt_ps2"], 1)
                k_ = (k0a if L == 0 else k1)[b]
                order = [(j, t) for t in range(tiles) for j in range(HPG)]
                for m, (j, t) in enumerate(order):
                    yield 3 + m * step // 4
                    if m == 0:
                        pe.wait_ge((ld_k0 if L == 0 else ld_k1)[b], 16 * 8 * use(p, s))
                        wait(pe, "a_qt", n)
                        if L == 1:
                            wait(pe, "a_qt2", i)
                    if m >= 2:
                        wait_part(pe, "a_r", n, step * (m - 1))
                    pe.matmul(QK[(1 + m) % 2][:, :], qt[b][:, t, P * j:P * (j + 1)],
                              k_[:, 4 * t:4 * t + 4, :].rearrange("p g t -> p (g t)"), start=True, stop=True)\
                      .then_inc(S["a_m"], step)
                yield 7
                wait_part(pe, "a_r", n, 8)
                if L == 0:
                    wait(pe, "a_q_hi2", n)
                    turn(QK[1], lambda j: q0b[:, j].rearrange("p g b -> p (g b)"), HPG).then_inc(S["a_mt_ps"], 1)
                else:
                    turn(QK[0], lambda j: q1[:, j, 0:4].rearrange("p g b -> p (g b)"), HPG).then_inc(S["a_mt_ps"], 1)
                    turn(QK[1], lambda j: q1[:, j, 4:8].rearrange("p g b -> p (g b)"), HPG).then_inc(S["a_mt_ps2"], 1)

            def attention_2(p, s, L):
                yield 0
                n, i, b = halves_index(p, s, L)
                tiles = G[L] // 4
                step = 8 // G[L]
                wait(pe, "a_mt", n)
                if L == 1:
                    wait(pe, "a_mt2", i)
                wait_before(pe, "a_out", n)
                for g in range(G[L]):
                    yield g // 2
                    if g >= 2:
                        wait_part(pe, "a_e", n, step * (g - 1))
                    o = PV[g % 2][:, :]
                    if L == 0:
                        pe.matmul(o, k0a[b][:, g, :], qt[b][:, 0, :], start=True, stop=False)
                        last = pe.matmul(o, k0b[b][:, g, :], qt[b][:, 1, :], start=False, stop=True)
                    else:
                        last = pe.matmul(o, k1[b][:, g, :], qt[b][:, g // 4, :], start=True, stop=True)
                    last.then_inc(S["a_s"], step)
                yield 4
                wait(pe, "v0_done" if L == 0 else "v1_done", i)
                vv = v0[b] if L == 0 else v1[s]
                wait_part(pe, "a_e", n, 8)
                for t in range(tiles):
                    for g in range(4):
                        last = pe.matmul(PV[t][BLK * g:BLK * (g + 1), :], vv[:, 4 * t + g, :], pt[:, 4 * t + g, :],
                                         start=True, stop=True)
                    last.then_inc(S["a_pv" if t == 0 else "a_pv2"], 1)
                yield 5
                wait(pe, "a_ot", n)
                turn(PV[1] if L == 0 else PV[0], lambda j: ot[:, 0, P * j:P * (j + 1)], HPG).then_inc(S["a_otT"], 1)
                if L == 1:
                    wait(pe, "a_ot2", i)
                    turn(PV[1], lambda j: ot[:, 1, P * j:P * (j + 1)], HPG).then_inc(S["a_otT2"], 1)
                else:
                    yield 6
                    wait(pe, "a_on", n)
                    turn(PV[0], lambda k: on[:, P * k:P * (k + 1)], KT).then_inc(S["a_onT"], 1)
                    yield 7
                    wait(pe, "a_aohi", i)
                    wait(pe, "a_aolo", i)
                    if isinstance(p, int) and p == 0 and s == 0:
                        pe.wait_ge(S["c_hi"], 2)
                        pe.wait_ge(S["c_lo"], 2)
                    for k in range(KT):
                        last = product(PV[1][:, 0:D], ao_hi[:, k, :], ao_lo[:, k, :], wc_hi[:, k, :], wc_lo[:, k, :],
                                       k == 0, k == KT - 1)
                    last.then_inc(S["a_proj"], 1)

            def gate_or_up(o, b, q, off, name):
                for k in range(KT):
                    w = w13_r[:, k, 2 * PAIR * q + off:2 * PAIR * q + off + PAIR]
                    last = product(o[:, 0:PAIR], at_hi[b][:, k, :], at_lo[b][:, k, :], w, None, k == 0, k == KT - 1)
                last.then_inc(S[f"{name}{q}"], 1)

            def ffn_1(p, s, L):
                yield 1
                n, i, b = halves_index(p, s, L)
                if isinstance(p, int) and p == 0 and s == 0:
                    if L == 0:
                        pe.wait_ge(S["c_hi"], 5)
                        pe.wait_ge(S["c_lo"], 5)
                    else:
                        pe.wait_ge(S["ld_w13"], 16)
                        pe.wait_ge(S["ld_w2"], 32)
                wait_before(pe, "f_h1" if (L if s else 1 - L) == 0 else "f_h0", n)
                wait(pe, "f_norm", n)
                turn(UP[0], lambda k: f_xn[:, P * k:P * (k + 1)], KT).then_inc(S["f_xt_ps"], 1)
                yield 2
                wait(pe, "f_at_hi", n)
                wait(pe, "f_at_lo", n)
                if L == 0:
                    for c in range(2):
                        yield (2, 4)[c]
                        for b_, off, name in ((0, 0, "f_g"), (1, I0, "f_u")):
                            if c:
                                wait(pe, "f_h0" if b_ else "f_sg0", n)
                            for k in range(KT):
                                w = slice(off + CH * c, off + CH * (c + 1))
                                last = product(UP[b_][:, :], at_hi[b][:, k, :], at_lo[b][:, k, :],
                                               up_hi[:, k, w], up_lo[:, k, w], k == 0, k == KT - 1)
                            last.then_inc(S[f"{name}{c}"], 1)
                else:
                    for k in range(KT):
                        last = product(UP[1][:, 0:E], at_hi[b][:, k, :], at_lo[b][:, k, :], gate_hi[:, k, :],
                                       gate_lo[:, k, :], k == 0, k == KT - 1)
                    last.then_inc(S["f_ro"], 1)
                    c0 = 2 * E * EI
                    for k in range(KT):
                        last = product(UP[0][:, 0:2 * EI], at_hi[b][:, k, :], at_lo[b][:, k, :],
                                       w13_r[:, k, c0:c0 + 2 * EI], None, k == 0, k == KT - 1)
                    last.then_inc(S["f_sh"], 1)
                    yield 3
                    wait(pe, "f_lg", i)
                    gate_or_up(UP[1], b, 0, PAIR, "f_u")
                    yield 5
                    wait(pe, "f_hs", i)
                    gate_or_up(UP[0], b, 0, 0, "f_g")

            def ffn_2(p, s, L):
                yield 0
                n, i, b = halves_index(p, s, L)

                def down(ks, w_hi, w_lo, first, last_):
                    for k in ks:
                        last = product(DOWN[1][:, 0:D], ht_hi[:, k, :], ht_lo[:, k, :], w_hi[:, k, :],
                                       None if w_lo is None else w_lo[:, k, :], k == first, k == last_)
                    return last

                if L == 0:
                    for c in range(2):
                        yield (2, 4)[c]
                        wait(pe, f"f_hm{c}", i)
                        if c:
                            wait(pe, "f_th0", n)
                            wait(pe, "f_tl0", n)
                        else:
                            wait_before(pe, "f_out", n)
                        turn(DOWN[0], lambda k: hid[b][:, CH * c + P * k:CH * c + P * (k + 1)], 4)\
                            .then_inc(S[f"f_t{c}"], 1)
                        if c:
                            down(range(0, 4), down_hi, down_lo, 0, I0 // P - 1)
                            yield 6
                            wait(pe, "f_th1", n)
                            wait(pe, "f_tl1", n)
                            down(range(4, 8), down_hi, down_lo, 0, I0 // P - 1).then_inc(S["f_y"], 1)
                else:
                    def turn_hidden(t, b_, count, m):
                        turn(DOWN[b_], lambda k: hid[b][:, CH * t + P * k:CH * t + P * (k + 1)], count)\
                            .then_inc(S[f"f_t{t}"], 1)

                    wait_before(pe, "f_out", n)
                    wait(pe, "f_hs", i)
                    turn_hidden(3, 1, 1, i)
                    yield 1
                    for q in range(1, 4):
                        yield q
                        if q > 1:
                            wait(pe, f"f_sg{q - 1}", n if q == 2 else i)
                        gate_or_up(DOWN[0], b, q, 0, "f_g")
                        if q == 1:
                            wait(pe, "f_th3", i)
                            wait(pe, "f_tl3", i)
                        else:
                            wait(pe, f"f_h{q - 1}", n if q == 2 else i)
                        gate_or_up(DOWN[1], b, q, PAIR, "f_u")
                    yield 4
                    wait(pe, "f_h3", i)
                    turn_hidden(0, 0, 4, n)
                    turn_hidden(1, 1, 4, n)
                    yield 5
                    wait(pe, "f_th0", n)
                    wait(pe, "f_tl0", n)
                    turn_hidden(2, 0, 4, i)
                    wait(pe, "f_th1", n)
                    wait(pe, "f_tl1", n)
                    down([NT1 - 1, *range(8)], w2_r, None, NT1 - 1, NT1 - 2)
                    yield 6
                    wait(pe, "f_th2", i)
                    wait(pe, "f_tl2", i)
                    down(range(8, 12), w2_r, None, NT1 - 1, NT1 - 2).then_inc(S["f_y"], 1)

            rounds(pe, (attention_1, attention_2, ffn_1, ffn_2))

        @block.vector
        def _(dve):
            kh, kl = up_lo[0:C, 0, 0:B * T], up_lo[0:C, 1, 0:B * T]
            kt_raw = work[0:C, 0:B * T]
            dve.wait_ge(S["c_kh"], 1)
            dve.tensor_tensor(kl, kt_raw, kh.bitcast(F32), ALU.subtract).then_inc(S["c_kl"], 1)
            for s in range(2):
                dve.memset(k0a[s][:, :, :].bitcast(F32), 0.0).then_inc(S["c_oh"], 1)
            dve.wait_ge(S["c_sel"], 3)
            for s in range(2):
                one_hot = [pt[:, h, :].rearrange("p (g t) -> p g t", g=4) for h in (0, 2)]
                dve.tensor_copy(k0b[s][:, :, :], one_hot[0]).then_inc(S["c_oh"], 1)
                for t in range(2):
                    last = dve.tensor_copy(k1[s][:, 4 * t:4 * t + 4, :], one_hot[1])
                last.then_inc(S["c_oh"], 1)
            dve.wait_ge(S["c_tg"], 1)
            dve.tensor_scalar(bcg[:, :], bcg[:, :], tg[:, 0:1], None, ALU.mult).then_inc(S["c_vec"], 1)
            dve.wait_ge(S["c_hi"], 2)
            dve.tensor_tensor(gate_lo[:, :, :], gate_raw[:, :, :], gate_hi[:, :, :].bitcast(F32), ALU.subtract)\
               .then_inc(S["c_lo"], 1)
            dve.tensor_tensor(wc_lo[:, :, :], work[:, 2048:2048 + 2 * D].rearrange("p (k n) -> p k n", k=KT),
                              wc_hi[:, :, :].bitcast(F32), ALU.subtract).then_inc(S["c_lo"], 1)

            def split_ffn_0_weights():
                for k in range(KT):
                    dve.wait_ge(S["c_hi"], 3 + k)
                    dve.tensor_tensor(up_lo[:, k, :], work[:, 2048 * k:2048 * (k + 1)], up_hi[:, k, :].bitcast(F32),
                                      ALU.subtract).then_inc(S["c_lo"], 1)
                dve.wait_ge(S["c_hi"], 5)
                dve.tensor_tensor(down_lo[:, :, :], work[:, 0:(I0 // P) * D].rearrange("p (k n) -> p k n", n=D),
                                  down_hi[:, :, :].bitcast(F32), ALU.subtract).then_inc(S["c_lo"], 1)
                dve.wait_ge(S["c_lo"], 5)
                for b in range(2):
                    dve.memset(hid[b][:, I1:HW], 0.0).then_inc(S["c_vec"], 1)

            def norm(pre, n, src, stat, mv, rs, xn):
                dve.bn_stats(stat[:, :], src[:, :]).then_inc(S[pre + "stats"], 1)
                wait_alone(dve, pre + "stats", n)
                dve.bn_aggr(mv[:, :], stat[:, :]).then_inc(S[pre + "mvd"], 1)

            def norm_apply(pre, n, src, mv, rs, xn):
                wait(dve, pre + "rstd", n)
                dve.tensor_scalar(xn[:, :], src[:, :], mv[:, 0:1], rs[:, :], ALU.subtract, ALU.mult)\
                   .then_inc(S[pre + "norm"], 1)

            def attention_1(p, s, L):
                yield 0
                n, i, b = halves_index(p, s, L)
                if L == 0:
                    src = x0[b]
                    dve.wait_ge(ld_x[b], 16 * use(p, s))
                else:
                    src = xr[s]
                    wait(dve, "f_out", n - NS)
                norm("a_", n, src, a_stat, a_mv, a_rs, a_xn)
                yield 1
                wait_before(dve, "a_q_lo", n)
                wait_before(dve, "a_q_hi2", n)
                norm_apply("a_", n, src, a_mv, a_rs, a_xn)
                step = 8 // G[L]
                order = [(j, t) for t in range(G[L] // 4) for j in range(HPG)]
                for m, (j, t) in enumerate(order):
                    yield 3 + m * step // 4
                    wait_part(dve, "a_m", n, step * (m + 1))
                    if L == 0:
                        o = q0b[:, j, :, HD0:HD0 + 1].rearrange("p g o -> p (g o)")
                    else:
                        o = q1[:, j, 4 * t:4 * t + 4, 3 * HD1:3 * HD1 + 1].rearrange("p g o -> p (g o)")
                    dve.tensor_reduce(o, QK[(1 + m) % 2][:, :].rearrange("p (g t) -> p g t", t=T), AX.X, ALU.max,
                                      negate=True).then_inc(S["a_r"], step)

            def attention_2(p, s, L):
                yield 5
                n, i, b = halves_index(p, s, L)
                d = HD[L]
                for t in range(G[L] // 4):
                    wait(dve, "a_otT" if t == 0 else "a_otT2", n if t == 0 else i)
                    o = (PV[1] if L == 0 else PV[t])[:, :].rearrange("p (j g b) -> p j g b", j=HPG, g=4)
                    r = rec[:, :, 4 * t:4 * t + 4]
                    dve.reciprocal(r, o[:, :, :, d:d + 1].rearrange("p j g o -> p j (g o)"))\
                       .then_inc(S["a_rec" if t == 0 else "a_rec2"], 1)
                    wait(dve, "a_rec" if t == 0 else "a_rec2", n if t == 0 else i)
                    ov = on[:, :].rearrange("p (g j d) -> p j g d", g=G[L], j=HPG)[:, :, 4 * t:4 * t + 4, :]
                    dve.tensor_tensor(ov, o[:, :, :, 0:d], r.unsqueeze(3).broadcast_to([P, HPG, 4, d]), ALU.mult)\
                       .then_inc(S["a_on" if t == 0 else "a_on2"], 1)
                if L == 0:
                    yield 6
                    wait(dve, "a_aohi", i)
                    dve.tensor_tensor(ao_lo[:, :, :], PV[0][:, 0:D].rearrange("p (k t) -> p k t", k=KT),
                                      ao_hi[:, :, :].bitcast(F32), ALU.subtract).then_inc(S["a_aolo"], 1)
                    yield 7
                    wait(dve, "a_proj", i)
                    wait(dve, "xb_done", i)
                    dve.scalar_tensor_tensor(out=xr[s][:, :], in0=PV[1][:, 0:D], scalar=tg[:, 0:1], in1=xr[s][:, :],
                                             op0=ALU.mult, op1=ALU.add).then_inc(S["a_out"], 1)
                else:
                    wait(dve, "a_on2", i)
                    dve.scalar_tensor_tensor(out=xr[s][:, :], in0=on[:, :], scalar=tg[:, 1:2], in1=xr[s][:, :],
                                             op0=ALU.mult, op1=ALU.add).then_inc(S["a_out"], 1)

            def expert_pair(o, b, q, m):
                wait(dve, f"f_sg{q}", m)
                wait(dve, f"f_u{q}", m)
                for k in range(2):
                    e = 2 * q + k
                    r = PAIR * (q % 2) + EI * k
                    last = dve.scalar_tensor_tensor(
                        out=hid[b][:, EI * e:EI * (e + 1)], in0=o[:, EI * k:EI * (k + 1)],
                        scalar=cw[b][:, e:e + 1], in1=sg[b][:, r:r + EI], op0=ALU.mult, op1=ALU.mult)
                last.then_inc(S[f"f_h{q}"], 1)

            def ffn_1(p, s, L):
                yield 0
                n, i, b = halves_index(p, s, L)
                src = xr[s]
                wait(dve, "a_out", n)
                norm("f_", n, src, f_stat, f_mv, f_rs, f_xn)
                yield 1
                norm_apply("f_", n, src, f_mv, f_rs, f_xn)
                wait(dve, "f_at_hi", n)
                dve.tensor_tensor(at_lo[b][:, :, :], UP[0][:, 0:D].rearrange("p (k t) -> p k t", k=KT),
                                  at_hi[b][:, :, :].bitcast(F32), ALU.subtract).then_inc(S["f_at_lo"], 1)
                if L == 0:
                    for c in range(2):
                        yield (3, 5)[c]
                        cols = slice(CH * c, CH * (c + 1))
                        wait(dve, f"f_sg{c}", n)
                        wait(dve, f"f_u{c}", n)
                        dve.tensor_tensor(hid[b][:, cols], UP[1][:, :], sg[b][:, cols], ALU.mult)\
                           .then_inc(S[f"f_h{c}"], 1)
                else:
                    yield 2
                    wait(dve, "f_ro", i)
                    dve.tensor_copy(lg[:, :], UP[1][:, 0:E]).then_inc(S["f_lg"], 1)
                    wait(dve, "f_lg", i)
                    dve.scalar_tensor_tensor(out=rt[:, 0, :], in0=lg[:, :], scalar=-1.0, in1=lg[:, :],
                                             op0=ALU.mult, op1=ALU.min).then_inc(S["f_r1"], 1)
                    yield 3
                    wait(dve, "f_r2", i)
                    dve.tensor_scalar(rt[:, 2, :], rt[:, 1, :], 1.0, None, ALU.add).then_inc(S["f_r3"], 1)
                    wait(dve, "f_r3", i)
                    dve.tensor_scalar(rt[:, 4, :], rt[:, 2, :], -1.0, 2.0 ** -23, ALU.add, ALU.max).then_inc(S["f_r0"], 1)
                    wait(dve, "f_r0", i)
                    dve.reciprocal(rt[:, 5, :], rt[:, 4, :])
                    dve.tensor_scalar(rt[:, 6, :], rt[:, 1, :], -0.5, 1.0, ALU.mult, ALU.add).then_inc(S["f_r5"], 1)
                    wait(dve, "f_r5", i)
                    dve.tensor_tensor(rt[:, 5, :], rt[:, 5, :], rt[:, 1, :], ALU.mult)
                    dve.tensor_tensor(rt[:, 6, :], rt[:, 6, :], rt[:, 1, :], ALU.mult).then_inc(S["f_r6"], 1)
                    yield 4
                    wait(dve, "f_r4", i)
                    wait(dve, "f_r6", i)
                    dve.tensor_tensor(rt[:, 5, :], rt[:, 5, :], rt[:, 3, :], ALU.mult).then_inc(S["f_r9"], 1)
                    wait(dve, "f_r9", i)
                    dve.tensor_tensor(rt[:, 6, :], rt[:, 6, :], rt[:, 5, :], ALU.max).then_inc(S["f_r10"], 1)
                    wait(dve, "f_r10", i)
                    dve.scalar_tensor_tensor(out=rt[:, 7, :], in0=lg[:, :], scalar=0.0, in1=rt[:, 6, :],
                                             op0=ALU.max, op1=ALU.add).then_inc(S["f_r7"], 1)
                    wait(dve, "f_sgs", i)
                    dve.tensor_tensor(hid[b][:, E * EI:I1], UP[0][:, EI:2 * EI], sg[b][:, 2 * PAIR:2 * PAIR + EI],
                                      ALU.mult)\
                       .then_inc(S["f_hs"], 1)
                    yield 5
                    wait(dve, "f_r8", i)
                    dve.tensor_tensor(rt[:, 9, :], rt[:, 8, :], gb[:, :], ALU.add).then_inc(S["f_r11"], 1)
                    wait(dve, "f_r11", i)
                    own = rt[:, 9, :].unsqueeze(2).broadcast_to([P, E, E])
                    other = rt[:, 9, :].unsqueeze(1).broadcast_to([P, E, E])
                    dve.tensor_tensor(cmp[:, 0], other, own, ALU.is_ge)
                    dve.tensor_tensor(cmp[:, 1], other, own, ALU.is_gt).then_inc(S["f_cmp2"], 1)
                    wait(dve, "f_cmp2", i)
                    dve.tensor_tensor(cmp[:, :, :, :], cmp[:, :, :, :], tie[:, :, :, :], ALU.mult)\
                       .then_inc(S["f_cmp3"], 1)
                    wait(dve, "f_cmp3", i)
                    dve.tensor_reduce(rank[:, :], cmp[:, :, :, :].rearrange("p a e f -> p e a f"), AX.XY, ALU.add)\
                       .then_inc(S["f_rank"], 1)
                    wait(dve, "f_rank", i)
                    dve.scalar_tensor_tensor(out=cw[b][:, :], in0=rank[:, :], scalar=1.5, in1=rt[:, 8, :],
                                             op0=ALU.is_lt, op1=ALU.mult).then_inc(S["f_cw"], 1)
                    yield 7
                    wait(dve, "f_cw", i)
                    expert_pair(UP[1], b, 0, n)

            def hidden_t(n, t, b, cols):
                wait(dve, f"f_th{t}", n)
                r = slice(4 * t, 4 * t + cols // P)
                dve.tensor_tensor(ht_lo[:, r, :], DOWN[b][:, 0:cols].rearrange("p (k t) -> p k t", t=P),
                                  ht_hi[:, r, :].bitcast(F32), ALU.subtract).then_inc(S[f"f_tl{t}"], 1)

            def ffn_2(p, s, L):
                yield 0
                n, i, b = halves_index(p, s, L)
                if L == 0:
                    for c in range(2):
                        yield c
                        cols = slice(CH * c, CH * (c + 1))
                        wait(dve, f"f_abs{c}", i)
                        a = sg[b][:, cols].rearrange("p (n a e) -> p n a e", a=2, e=2)
                        dve.tensor_tensor(pmax[:, :, :], a[:, :, :, 0], a[:, :, :, 1], ALU.max)
                        dve.tensor_tensor(pmin[:, :, :], a[:, :, :, 0], a[:, :, :, 1], ALU.min)
                        dve.tensor_tensor(lose[:, :, :, 0], a[:, :, :, 0], a[:, :, :, 1], ALU.is_lt)
                        dve.tensor_tensor(lose[:, :, :, 1], a[:, :, :, 0], a[:, :, :, 1], ALU.is_ge)\
                           .then_inc(S["f_pairs"], 1)
                        dve.wait_ge(S["f_pairs"], 2 * i + 1 + c)
                        dve.tensor_tensor(both[:, 0, :], pmin[:, :, 0], pmax[:, :, 1], ALU.is_ge)
                        dve.tensor_tensor(both[:, 1, :], pmin[:, :, 1], pmax[:, :, 0], ALU.is_gt)\
                           .then_inc(S["f_cmp"], 1)
                        dve.wait_ge(S["f_cmp"], 2 * i + 1 + c)
                        dve.tensor_tensor(lead[:, :, 0], both[:, 0, :], both[:, 1, :], ALU.subtract)
                        dve.tensor_tensor(lead[:, :, 1], both[:, 1, :], both[:, 0, :], ALU.subtract)\
                           .then_inc(S["f_lead"], 1)
                        dve.wait_ge(S["f_lead"], 2 * i + 1 + c)
                        dve.tensor_tensor(keep[:, c, :].rearrange("p (n a e) -> p n a e", a=2, e=2),
                                          lead[:, :, :].unsqueeze(3).broadcast_to([P, NG, 2, 2]), lose[:, :, :, :],
                                          ALU.is_ge).then_inc(S[f"f_keep{c}"], 1)
                    for t in range(2):
                        yield (3, 5)[t]
                        hidden_t(n, t, 0, 4 * P)
                    yield 7
                    wait(dve, "f_y", n)
                    dve.scalar_tensor_tensor(out=xr[s][:, :], in0=DOWN[1][:, 0:D], scalar=tg[:, 2:3], in1=xr[s][:, :],
                                             op0=ALU.mult, op1=ALU.add).then_inc(S["f_out"], 1)
                else:
                    hidden_t(i, 3, 1, P)
                    for q in range(1, 4):
                        yield q
                        expert_pair(DOWN[1], b, q, n if q < 2 else i)
                    yield 4
                    for t in range(2):
                        hidden_t(n, t, t, 4 * P)
                    yield 5
                    hidden_t(i, 2, 0, 4 * P)
                    yield 7
                    wait(dve, "f_y", n)
                    if not (isinstance(p, int) and p == 0 and s < 2):
                        dve.wait_ge(st_y[b], 16 * (use(p, s) - 1))
                    dve.scalar_tensor_tensor(out=y[b][:, :], in0=DOWN[1][:, 0:D], scalar=tg[:, 3:4], in1=xr[s][:, :],
                                             op0=ALU.mult, op1=ALU.add).then_inc(S["f_out"], 1)

            rounds(dve, (attention_1, attention_2, ffn_1, ffn_2), split_ffn_0_weights)


_IN = ["x", "ctx_kv", "ctx_t", "g_x", "g_f", "wc_t", "bc", "w_up", "w_down", "gate_w_t", "gate_b", "w13", "w2"]


def kernel(x, ctx_512, g_xattn, g_ffn, L0_xattn_Wc, L0_xattn_bc, L0_ffn_w_gate, L0_ffn_w_up, L0_ffn_w_down,
           L1_ffn_gate_w, L1_ffn_gate_b, L1_ffn_w1, L1_ffn_w2, L1_ffn_w3, L1_ffn_sw1, L1_ffn_sw2, L1_ffn_sw3):
    import concourse.bacc as bacc
    from concourse.bass_utils import run_bass_kernel_spmd

    E, EI, D = L1_ffn_w1.shape
    up = []
    for q in range(E // 2):
        up += [L1_ffn_w1[2 * q], L1_ffn_w1[2 * q + 1], L1_ffn_w3[2 * q], L1_ffn_w3[2 * q + 1]]
    w13 = np.concatenate(up + [L1_ffn_sw1, L1_ffn_sw3], axis=0).T
    w2 = np.concatenate([L1_ffn_w2.transpose(0, 2, 1).reshape(E * EI, D), np.asarray(L1_ffn_sw2).T], axis=0)
    arrays = {
        "x": x, "ctx_kv": ctx_512, "ctx_t": ctx_512.transpose(2, 0, 1).reshape(ctx_512.shape[2], -1),
        "g_x": g_xattn, "g_f": g_ffn, "wc_t": L0_xattn_Wc.T, "bc": L0_xattn_bc,
        "w_up": np.concatenate([L0_ffn_w_gate, L0_ffn_w_up], axis=1), "w_down": L0_ffn_w_down,
        "gate_w_t": L1_ffn_gate_w.T, "gate_b": L1_ffn_gate_b, "w13": w13, "w2": w2,
    }
    arrays = {f"in_{k}": np.ascontiguousarray(v) for k, v in arrays.items()}
    nc = bacc.Bacc("TRN2", target_bir_lowering=False, num_devices=1)
    args = [nc.dram_tensor(f"in_{k}", arrays[f"in_{k}"].shape, mybir.dt.from_np(arrays[f"in_{k}"].dtype),
                           kind="ExternalInput").ap() for k in _IN]
    out = nc.dram_tensor("out", arrays["in_x"].shape, F32, kind="ExternalOutput").ap()
    flamingo_block(nc, *args, out)
    return run_bass_kernel_spmd(nc, [arrays], core_ids=[0]).results[0]["out"]
```

```python
from contextlib import ExitStack

import numpy as np

import concourse.bass as bass
from concourse import mybir

ALU = mybir.AluOpType
ACT = mybir.ActivationFunctionType
F32 = mybir.dt.float32
F32R = mybir.dt.float32r
BF16 = mybir.dt.bfloat16
AX = mybir.AxisListType



def flamingo_block(nc, x, ctx_kv, ctx_t, g_x, g_f, wc_t, bc, w_up, w_down, gate_w_t, gate_b, w13, w2, out):
    B, T, D = x.shape
    C = ctx_kv.shape[2]
    P = 128
    assert T == P and D == 2 * P and C == 64
    KT = D // P
    G0, HD0 = 4, 16
    G1, HD1 = 8, 8
    HPG = 4
    BLK = 32
    I0 = w_down.shape[0]
    E = gate_b.shape[0]
    EI = 176
    I1 = (E + 1) * EI
    NT1 = -(-I1 // P)
    PAIR = 2 * EI
    EPS = 1e-5
    NS = 4
    RND = B // NS
    assert I0 == 8 * P and E == 8

    ctx = ExitStack()
    with ctx:
        def sb(name, shape, dt=F32):
            return ctx.enter_context(nc.sbuf_tensor(name, shape, dt))

        def sem(name):
            return ctx.enter_context(nc.semaphore(name))

        up_hi = sb("up_hi", [P, KT, 2 * I0], F32R)
        up_lo = sb("up_lo", [P, KT, 2 * I0], F32R)
        down_hi = sb("down_hi", [P, I0 // P, D], F32R)
        down_lo = sb("down_lo", [P, I0 // P, D], F32R)
        wc_hi = sb("wc_hi", [P, KT, D], F32R)
        wc_lo = sb("wc_lo", [P, KT, D], F32R)
        w13_r = sb("w13_r", [P, KT, 2 * I1], F32R)
        gate_hi = sb("gate_hi", [P, KT, E], F32R)
        gate_lo = sb("gate_lo", [P, KT, E], F32R)
        w2_r = sb("w2_r", [P, NT1, D], F32R)
        gate_raw = sb("gate_raw", [P, KT, E])
        gb = sb("gb", [P, E])
        bcg = sb("bcg", [P, D])
        graw = sb("graw", [P, 4])
        tg = sb("tg", [P, 4])
        ident = sb("ident", [P, P])
        neg_half = sb("neg_half", [P, 1])
        half = sb("half", [P, E])
        tie = sb("tie", [P, 2, E, E], BF16)

        xr = [sb(f"xr_{s}", [P, D]) for s in range(NS)]
        v1 = [sb(f"v1_{s}", [P, G1, BLK]) for s in range(NS)]

        x0 = [sb(f"x0_{b}", [P, D]) for b in range(2)]
        y = sb("y", [P, D])
        ct = [sb(f"ct_{b}", [P, C]) for b in range(2)]
        v0 = [sb(f"v0_{b}", [P, G0, BLK]) for b in range(2)]
        k0a = [sb(f"k0a_{s}", [P, G0, T], F32R) for s in range(2)]
        k0b = [sb(f"k0b_{s}", [P, G0, T], F32R) for s in range(2)]
        k1 = [sb(f"k1_{s}", [P, G1, T], F32R) for s in range(2)]

        a_stat = sb("a_stat", [P, 6])
        a_mv = sb("a_mv", [P, 2])
        a_ve = sb("a_ve", [P, 1])
        a_rs = sb("a_rs", [P, 1])
        a_xn = sb("a_xn", [P, D])
        q0a = sb("q0a", [P, HPG, G0, BLK])
        q0b = sb("q0b", [P, HPG, G0, BLK])
        q1 = sb("q1", [P, HPG, G1, BLK])
        qt = [sb(f"qt{b}", [P, 2, HPG * T], F32R) for b in range(2)]
        pt = sb("pt", [P, G1, HPG * T])
        ot = sb("ot", [P, 2, HPG * T])
        rec = sb("rec", [P, HPG, G1])
        on = sb("on", [P, D])
        ao_hi = sb("ao_hi", [P, KT, P], F32R)
        ao_lo = sb("ao_lo", [P, KT, P], F32R)

        f_stat = sb("f_stat", [P, 6])
        f_mv = sb("f_mv", [P, 2])
        f_ve = sb("f_ve", [P, 1])
        f_rs = sb("f_rs", [P, 1])
        f_xn = sb("f_xn", [P, D])
        at_hi = [sb(f"at_hi{b}", [P, KT, P], F32R) for b in range(2)]
        at_lo = [sb(f"at_lo{b}", [P, KT, P], F32R) for b in range(2)]
        HW = NT1 * P
        work = sb("work", [P, 2 * HW + 2 * I0])
        hid = [work[:, HW * b:HW * (b + 1)] for b in range(2)]
        sg = [work[:, 2 * HW + I0 * b:2 * HW + I0 * (b + 1)] for b in range(2)]
        ht_hi = sb("ht_hi", [P, NT1, P], F32R)
        ht_lo = sb("ht_lo", [P, NT1, P], F32R)
        CH = 512
        NG = CH // 4
        pmax = sb("pmax", [P, NG, 2])
        pmin = sb("pmin", [P, NG, 2])
        lose = sb("lose", [P, NG, 2, 2], BF16)
        both = sb("both", [P, 2, NG], BF16)
        lead = sb("lead", [P, NG, 2], BF16)
        keep = sb("keep", [P, 2, CH], BF16)
        rt = sb("rt", [P, 10, E])
        cmp = sb("cmp", [P, 2, E, E], BF16)
        rank = sb("rank", [P, E])
        cw = [sb(f"cw{b}", [P, E]) for b in range(2)]

        half_bank = [[ctx.enter_context(nc.psum_tensor(f"bank{h}{b}", [P, 512], F32)) for b in range(2)]
                     for h in range(4)]
        QK, PV, UP, DOWN = half_bank

        kd0a = nc.dram_tensor("kd0a", (G0, 2, HD0, B * T), F32, kind="Internal").ap()
        kd0b = nc.dram_tensor("kd0b", (G0, HD0, B * T), F32, kind="Internal").ap()
        kd1 = nc.dram_tensor("kd1", (G1, 3, HD1, B * T), F32, kind="Internal").ap()

        names = """
        ld_kt ld_small ld_up ld_down ld_wc ld_w13 ld_w2 scratch_k0 scratch_k1
        c_mem c_sel c_oh c_tg c_hi c_kh c_kl c_lo c_vec
        xb_done v0_done v1_done
        a_stats a_mvd a_veps a_rstd a_norm a_q_hi a_q_hi2 a_q_lo a_qt_ps a_qt_ps2 a_qt a_qt2
        a_m a_r a_mt_ps a_mt_ps2 a_mt a_mt2 a_mclear a_s a_e
        a_pv a_pv2 a_ot a_ot2 a_otT a_otT2 a_rec a_rec2 a_on a_on2 a_onT a_aohi a_aolo a_proj a_out
        f_stats f_mvd f_veps f_rstd f_norm f_xt_ps f_at_hi f_at_lo
        f_g0 f_u0 f_g1 f_u1 f_sg0 f_sg1 f_h0 f_h1
        f_gx1 f_ux1 f_sgx1 f_hx1 f_gx2 f_ux2 f_sgx2 f_hx2 f_gx3 f_ux3 f_sgx3 f_hx3
        f_abs0 f_abs1 f_pairs0 f_pairs1 f_first0 f_first1 f_second0 f_second1 f_cmp0 f_cmp1 f_lead0 f_lead1 f_cmp2 f_cmp3 f_rank f_keep0 f_keep1 f_hm0 f_hm1
        f_sh f_ro f_lg f_sgs f_hs f_r2 f_r3 f_r4 f_r5 f_r6 f_r7 f_r8 f_r9 f_r11 f_cw
        f_t0 f_t1 f_t2 f_t3 f_th0 f_th1 f_th2 f_th3 f_tl0 f_tl1 f_tl2 f_tl3 f_y f_out
        """.split()
        S = {n: sem(n) for n in names}
        ld_x = [sem(f"ld_x{b}") for b in range(2)]
        ld_ct = [sem(f"ld_ct{b}") for b in range(2)]
        ld_k0 = [sem(f"ld_k0{s}") for s in range(2)]
        ld_k1 = [sem(f"ld_k1{s}") for s in range(2)]
        st_y = sem("st_y")

        def wait(eng, name, n):
            eng.wait_ge(S[name], n + 1)

        def wait_before(eng, name, n, back=1):
            if not (isinstance(n, int) and n < back):
                eng.wait_ge(S[name], n + 1 - back)

        def wait_part(eng, name, n, k):
            eng.wait_ge(S[name], 8 * n + k)

        def wait_alone(eng, name, n, back=0):
            if isinstance(n, int) and n < back:
                return
            count = n + 1 - back
            if not isinstance(count, int):
                count = eng.snap(eng.to_reg(count))
            eng.wait_ge(S["c_mem"], 15)
            eng.wait_ge(S[name], count)

        PLACE = {
            (0, 0): [18, 31, 45, 51, 54, 56, 61, 72, 72, 72, 76],
            (0, 1): [4, 17, 28, 36, 38, 42, 50, 55, 66, 74, 75],
            (1, 0): [0, 0, 8, 10, 14, 15, 26, 26, 27, 47, 48, 59, 70, 78, 83],
            (1, 1): [1, 3, 6, 6, 19, 24, 24, 29, 33, 37, 46, 57, 57, 65, 67],
            (2, 0): [2, 16, 20, 30, 41, 43, 44, 68, 68, 68, 68, 68, 68, 81, 80],
            (2, 1): [7, 21, 23, 32, 35, 39, 62, 64, 64, 64, 69, 77, 82, 84, 87],
            (3, 0): [12, 13, 22, 25, 34, 58, 73, 73, 86, 86],
            (3, 1): [5, 5, 9, 11, 40, 40, 49, 52, 53, 53, 53, 60, 60, 63, 71, 71, 71, 79, 79, 79, 85],
        }

        def alternate(*halves):
            at = {h: (PLACE[k][next(h)], k[0]) for k, h in halves}
            layer = {h: k for k, h in halves}
            while at:
                h = min(at, key=at.get)
                step = next(h, None)
                if step is None:
                    del at[h]
                else:
                    at[h] = (PLACE[layer[h]][step], layer[h][0])

        def rounds(eng, halves, weights=None):
            def slot(p, t, first=0):
                now = []
                for h in range(first, 4):
                    q, k = (p, t - h) if t >= h else (p - 1, t - h + 2 * NS)
                    if not (isinstance(q, int) and q < 0):
                        now.append(((h, k // NS), halves[h](q, k % NS, k // NS)))
                alternate(*now)

            def body(p):
                for t in range(2 * NS):
                    slot(p, t)
                    if weights and isinstance(p, int) and t < 4:
                        weights(t)

            body(0)
            with eng.Fori(1, RND) as p:
                body(p)
            for t in range(3):
                slot(RND, t, first=t + 1)

        def use(p, s):
            return NS // 2 * p + s // 2 + 1

        def halves_index(p, s, L):
            return 2 * NS * p + NS * L + s, NS * p + s, s % 2

        kt_raw = pt[0:C, 4:8, :].rearrange("p g t -> p (g t)")
        kh, kl = (t[0:C, :, :].rearrange("p k n -> p (k n)") for t in (down_hi, down_lo))
        wc_raw = ot[:, 0, :].rearrange("p (k n) -> p k n", k=KT)
        up_raw = [work[:, 2 * I0 * k:2 * I0 * (k + 1)] for k in range(KT)]
        down_raw = pt[:, 4:8, :].rearrange("p g (k n) -> p (g k) n", n=D)

        block = ctx.enter_context(nc.Block())
        G = [G0, G1]
        HD = [HD0, HD1]

        @block.sync
        def _(sp):
            sp.dma_start(kt_raw, ctx_t).then_inc(S["ld_kt"], 16)
            sp.dma_start(graw[:, 0:2], g_x.partition_broadcast(P)).then_inc(S["ld_small"], 16)
            sp.dma_start(graw[:, 2:4], g_f.partition_broadcast(P)).then_inc(S["ld_small"], 16)
            sp.dma_start(bcg[:, :], bc.partition_broadcast(P)).then_inc(S["ld_small"], 16)
            sp.dma_start(gb[:, :], gate_b.partition_broadcast(P)).then_inc(S["ld_small"], 16)
            sp.dma_start(gate_raw[:, :, :], gate_w_t.rearrange("(k p) e -> p k e", p=P)).then_inc(S["ld_small"], 16)

            def load_x(i, s):
                sp.dma_start(x0[s][:, :], x[i]).then_inc(ld_x[s], 16)
                sp.dma_start(ct[s][:, :], ctx_kv[i]).then_inc(ld_ct[s], 16)

            def load_k0(i, s):
                for g in range(G0):
                    sp.dma_start(k0a[s][BLK * g:BLK * (g + 1), g, :].bitcast(F32),
                                 kd0a[g].rearrange("a d (b t) -> (a d) b t", t=T)[:, i, :]).then_inc(ld_k0[s], 16)
                    sp.dma_start(k0b[s][BLK * g:BLK * g + HD0, g, :].bitcast(F32),
                                 kd0b[g].rearrange("d (b t) -> d b t", t=T)[:, i, :]).then_inc(ld_k0[s], 16)

            def load_k1(i, s):
                for g in range(G1):
                    r = BLK * (g % 4)
                    sp.dma_start(k1[s][r:r + 3 * HD1, g, :].bitcast(F32),
                                 kd1[g].rearrange("a d (b t) -> (a d) b t", t=T)[:, i, :]).then_inc(ld_k1[s], 16)

            for s in range(2):
                load_x(s, s)
            sp.wait_ge(S["c_kh"], 1)
            for g in range(G0):
                for a in range(2):
                    sp.dma_start(kd0a[g, a], kh[HD0 * g:HD0 * (g + 1), :].bitcast(F32)).then_inc(S["scratch_k0"], 16)
            sp.wait_ge(S["c_kl"], 1)
            sp.dma_start(kd0b.rearrange("g d n -> (g d) n"), kl.bitcast(F32)).then_inc(S["scratch_k0"], 16)
            sp.wait_ge(S["scratch_k0"], 16 * (2 * G0 + 1))
            sp.wait_ge(S["c_oh"], 3 * 2)
            for s in range(2):
                load_k0(s, s)
            sp.dma_start(down_raw, w_down.rearrange("(k p) n -> p k n", p=P)).then_inc(S["ld_down"], 16)
            for g in range(G1):
                for a in range(3):
                    part = (kh, kh, kl)[a]
                    sp.dma_start(kd1[g, a], part[HD1 * g:HD1 * (g + 1), :].bitcast(F32)).then_inc(S["scratch_k1"], 16)
            sp.wait_ge(S["scratch_k1"], 16 * 3 * G1)
            for s in range(2):
                load_k1(s, s)

            def store(p, s):
                wait(sp, "f_out", 2 * NS * p + NS + s)
                sp.dma_start(out[NS * p + s], y[:, :]).then_inc(st_y, 16)

            def body(p, last=False):
                for s in range(NS):
                    n, i, b = halves_index(p, s, 0)
                    if not (isinstance(p, int) and p == 0):
                        store(p - 1, s)
                    if not (last and s >= 2):
                        wait(sp, "a_norm", n)
                        wait(sp, "xb_done", i)
                        wait(sp, "v0_done", i)
                        wait(sp, "v1_done", i)
                        load_x(i + 2, b)
                    if not (last and s >= 2):
                        wait_part(sp, "a_s", n, 8)
                        load_k0(i + 2, b)
                for s in range(NS):
                    n, i, b = halves_index(p, s, 1)
                    if not (last and s >= 2):
                        wait_part(sp, "a_s", n, 8)
                        load_k1(i + 2, b)

            body(0)
            with sp.Fori(1, RND - 1) as p:
                body(p)
            body(RND - 1, last=True)
            for s in range(NS):
                store(RND - 1, s)
            sp.wait_ge(st_y, 16 * B)

        @block.gpsimd
        def _(pool):
            for t in (q0a, q0b, q1):
                pool.memset(t[:, :, :, :], 0.0).then_inc(S["c_mem"], 1)
            for t in (pt[:, 0:4, :], w2_r[:, NT1 - 1, :].bitcast(F32)):
                pool.memset(t, 0.0).then_inc(S["c_mem"], 1)
            for t in (*v0, *v1):
                pool.memset(t[:, :, :], 0.0).then_inc(S["c_mem"], 1)
            pool.memset(ident[:, :], 0.0).then_inc(S["c_mem"], 1)
            pool.memset(neg_half[:, :], -0.5).then_inc(S["c_mem"], 1)
            pool.memset(half[:, :], 0.5).then_inc(S["c_mem"], 1)
            pool.memset(tie[:, :, :, :], 0.0).then_inc(S["c_mem"], 1)
            pool.wait_ge(S["c_mem"], 15)
            pool.affine_select(out=ident[:, :], in_=ident[:, :], compare_op=ALU.not_equal, fill=1.0,
                               base=0, pattern=[[-1, P]], channel_multiplier=1).then_inc(S["c_sel"], 1)
            for half_, row in ((0, HD0), (2, 3 * HD1)):
                v = pt[:, half_, :].rearrange("p (g t) -> p g t", g=4)
                pool.affine_select(out=v, in_=v, compare_op=ALU.not_equal, fill=1.0, base=-row,
                                   pattern=[[-BLK, 4], [0, T]], channel_multiplier=1).then_inc(S["c_sel"], 1)
            for t, d in (*((t, HD0) for t in v0), *((t, HD1) for t in v1)):
                pool.memset(t[:, :, d:d + 1], 1.0).then_inc(S["c_sel"], 1)
            pool.affine_select(out=tie[:, 0], in_=tie[:, 0], compare_op=ALU.is_ge, fill=1.0,
                               base=0, pattern=[[-1, E], [1, E]], channel_multiplier=0).then_inc(S["c_sel"], 1)
            pool.affine_select(out=tie[:, 1], in_=tie[:, 1], compare_op=ALU.is_ge, fill=1.0,
                               base=0, pattern=[[1, E], [-1, E]], channel_multiplier=0).then_inc(S["c_sel"], 1)
            pool.wait_ge(S["c_vec"], 1)

            def rstd(pre, n, mv, ve, rs):
                wait_alone(pool, pre + "mvd", n)
                pool.tensor_scalar(ve[:, :], mv[:, 1:2], EPS, None, ALU.add).then_inc(S[pre + "veps"], 1)
                wait(pool, pre + "veps", n)
                pool.tensor_tensor(rs[:, :], ve[:, :], neg_half[:, :], ALU.pow).then_inc(S[pre + "rstd"], 1)

            def attention_1(p, s, L):
                yield 0
                n, i, b = halves_index(p, s, L)
                rstd("a_", n, a_mv, a_ve, a_rs)
                yield 1
                wait(pool, "a_q_hi", n)
                d = HD[L]
                q = q0a if L == 0 else q1
                xv = a_xn[:, :].rearrange("p (g j d) -> p j g d", g=G[L], j=HPG)
                pool.tensor_tensor(q[:, :, :, d:2 * d], xv, q[:, :, :, 0:d], ALU.subtract).then_inc(S["a_q_lo"], 1)
                yield 2
                if L == 0:
                    pool.wait_ge(ld_x[b], 16 * use(p, s))
                    wait_before(pool, "f_out", n, NS)
                    pool.tensor_tensor(xr[s][:, :], x0[b][:, :], bcg[:, :], ALU.add).then_inc(S["xb_done"], 1)
                    wait_alone(pool, "a_pv", n, 2 if s >= 2 else 2 + NS)
                    pool.wait_ge(ld_ct[b], 16 * use(p, s))
                    pool.tensor_copy(v0[b][:, :, 0:HD0], ct[b][:, :].rearrange("p (g d) -> p g d", g=G0))\
                        .then_inc(S["v0_done"], 1)
                    wait_alone(pool, "a_pv2", i, NS)
                    pool.tensor_copy(v1[s][:, :, 0:HD1], ct[b][:, :].rearrange("p (g d) -> p g d", g=G1))\
                        .then_inc(S["v1_done"], 1)

            def attention_2(p, s, L):
                yield 1
                n, i, b = halves_index(p, s, L)
                if L == 1:
                    wait_alone(pool, "a_mt_ps2", i)
                    pool.memset(q1[:, :, :, 3 * HD1:3 * HD1 + 1], 0.0).then_inc(S["a_mclear"], 1)

            def losers_and_leads(c, i):
                wait_alone(pool, f"f_first{c}", i)
                pool.tensor_scalar(lose[:, :, :, 1], lose[:, :, :, 0], -1.0, 1.0, ALU.mult, ALU.add)\
                    .then_inc(S[f"f_second{c}"], 1)
                wait(pool, f"f_cmp{c}", i)
                pool.tensor_tensor(lead[:, :, 0], both[:, 0, :], both[:, 1, :], ALU.subtract)
                pool.tensor_tensor(lead[:, :, 1], both[:, 1, :], both[:, 0, :], ALU.subtract)\
                    .then_inc(S[f"f_lead{c}"], 1)

            def drop(c, i, b):
                wait(pool, f"f_keep{c}", i)
                h = hid[b][:, CH * c:CH * (c + 1)]
                pool.tensor_tensor(h, h, keep[:, c, :], ALU.mult).then_inc(S[f"f_hm{c}"], 1)

            def ffn_1(p, s, L):
                yield 0
                n, i, b = halves_index(p, s, L)
                rstd("f_", n, f_mv, f_ve, f_rs)
                if L == 0:
                    yield 10
                    losers_and_leads(0, i)
                    yield 13
                    drop(0, i, b)
                if L == 1:
                    yield 6
                    wait_alone(pool, "f_r2", i)
                    pool.tensor_scalar(rt[:, 2, :], rt[:, 1, :], 1.0, None, ALU.add).then_inc(S["f_r3"], 1)
                    wait_alone(pool, "f_r3", i)
                    pool.tensor_scalar(rt[:, 4, :], rt[:, 2, :], -1.0, None, ALU.add).then_inc(S["f_r5"], 1)
                    wait(pool, "f_r5", i)
                    pool.tensor_tensor(rt[:, 5, :], rt[:, 1, :], rt[:, 4, :], ALU.subtract).then_inc(S["f_r6"], 1)
                    wait(pool, "f_r6", i)
                    pool.tensor_tensor(rt[:, 6, :], rt[:, 5, :], rt[:, 7, :], ALU.add).then_inc(S["f_r9"], 1)
                    yield 9
                    wait(pool, "f_r4", i)
                    wait(pool, "f_r9", i)
                    pool.tensor_tensor(rt[:, 6, :], rt[:, 6, :], rt[:, 3, :], ALU.add).then_inc(S["f_r7"], 1)
                    wait(pool, "f_r7", i)
                    pool.tensor_tensor(rt[:, 8, :], rt[:, 6, :], half[:, :], ALU.pow).then_inc(S["f_r8"], 1)
                    wait(pool, "f_r8", i)
                    pool.tensor_tensor(rt[:, 9, :], rt[:, 8, :], gb[:, :], ALU.add).then_inc(S["f_r11"], 1)

            def ffn_2(p, s, L):
                yield 0
                n, i, b = halves_index(p, s, L)
                if L == 0:
                    losers_and_leads(1, i)
                    yield 3
                    drop(1, i, b)

            def load_ffn_1_weights(t):
                if t == 1:
                    pool.dma_start(w13_r[:, :, :], w13.rearrange("(k p) n -> p k n", p=P)).then_inc(S["ld_w13"], 16)
                if t == 3:
                    full = (NT1 - 1) * P
                    pool.dma_start(w2_r[:, 0:NT1 - 1, :], w2[0:full].rearrange("(k p) n -> p k n", p=P))\
                        .then_inc(S["ld_w2"], 16)
                    pool.dma_start(w2_r[0:I1 - full, NT1 - 1, :], w2[full:I1]).then_inc(S["ld_w2"], 16)

            rounds(pool, (attention_1, attention_2, ffn_1, ffn_2), load_ffn_1_weights)

        @block.scalar
        def _(act):
            act.dma_start(wc_raw, wc_t.rearrange("(k p) n -> p k n", p=P)).then_inc(S["ld_wc"], 16)
            act.wait_ge(S["ld_kt"], 16)
            act.activation(kh, kt_raw, ACT.Copy).then_inc(S["c_kh"], 1)
            for k in range(KT):
                act.dma_start(up_raw[k], w_up[k * P:(k + 1) * P, :]).then_inc(S["ld_up"], 16)
            act.wait_ge(S["ld_small"], 16 * 5)
            act.activation(tg[:, :], graw[:, :], ACT.Tanh).then_inc(S["c_tg"], 1)
            act.activation(gate_hi[:, :, :], gate_raw[:, :, :], ACT.Copy).then_inc(S["c_hi"], 1)
            act.wait_ge(S["ld_wc"], 16)
            act.activation(wc_hi[:, :, :], wc_raw, ACT.Copy).then_inc(S["c_hi"], 1)

            def round_ffn_0_weights(t):
                if t == 0:
                    act.wait_ge(S["ld_up"], 16 * KT)
                    for k in range(KT):
                        act.activation(up_hi[:, k, :], up_raw[k], ACT.Copy).then_inc(S["c_hi"], 1)
                if t == 2:
                    act.wait_ge(S["scratch_k1"], 16 * 3 * G1)
                    act.wait_ge(S["ld_down"], 16)
                    act.activation(down_hi[:, :, :], down_raw, ACT.Copy).then_inc(S["c_hi"], 1)

            def attention_1(p, s, L):
                yield 1
                n, i, b = halves_index(p, s, L)
                d = HD[L]
                wait(act, "a_norm", n)
                xv = a_xn[:, :].rearrange("p (g j d) -> p j g d", g=G[L], j=HPG)
                wait_before(act, "a_mt_ps", n)
                if L and s:
                    wait(act, "a_mt_ps2", i - 1)
                if L == 0:
                    act.activation(q0a[:, :, :, 0:d].bitcast(F32R), xv, ACT.Copy).then_inc(S["a_q_hi"], 1)
                    act.activation(q0b[:, :, :, 0:d].bitcast(F32R), xv, ACT.Copy).then_inc(S["a_q_hi2"], 1)
                else:
                    act.activation(q1[:, :, :, 0:d].bitcast(F32R), xv, ACT.Copy).then_inc(S["a_q_hi"], 1)
                    act.activation(q1[:, :, :, 2 * d:3 * d].bitcast(F32R), xv, ACT.Copy).then_inc(S["a_q_hi2"], 1)
                yield 2
                wait(act, "a_qt_ps", n)
                act.activation(qt[b][:, 0, :], QK[0][:, :], ACT.Copy).then_inc(S["a_qt"], 1)
                if L == 1:
                    wait(act, "a_qt_ps2", i)
                    act.activation(qt[b][:, 1, :], QK[1][:, :], ACT.Copy).then_inc(S["a_qt2"], 1)

            def attention_2(p, s, L):
                yield 0
                n, i, b = halves_index(p, s, L)
                yield 1
                wait(act, "a_mt_ps", n)
                if L == 0:
                    act.activation(qt[b][:, 1, :], PV[0][:, :], ACT.Copy).then_inc(S["a_mt"], 1)
                else:
                    act.activation(qt[b][:, 0, :], PV[0][:, :], ACT.Copy).then_inc(S["a_mt"], 1)
                    wait(act, "a_mt_ps2", i)
                    act.activation(qt[b][:, 1, :], PV[1][:, :], ACT.Copy).then_inc(S["a_mt2"], 1)
                step = 8 // G[L]
                for g in range(G[L]):
                    yield 2 + g * step
                    wait_part(act, "a_s", n, step * (g + 1))
                    act.activation(pt[:, g, :], PV[g % 2][:, :], ACT.Exp, scale=float(HD[L]) ** -0.5)\
                       .then_inc(S["a_e"], step)
                yield 10
                wait(act, "a_pv", n)
                act.activation(ot[:, 0, :], PV[0][:, :], ACT.Copy).then_inc(S["a_ot"], 1)
                if L == 1:
                    wait(act, "a_pv2", i)
                    act.activation(ot[:, 1, :], PV[1][:, :], ACT.Copy).then_inc(S["a_ot2"], 1)
                yield 12
                if L == 0:
                    wait(act, "a_onT", i)
                    act.activation(ao_hi[:, :, :], PV[0][:, 0:D].rearrange("p (k t) -> p k t", k=KT), ACT.Copy)\
                       .then_inc(S["a_aohi"], 1)

            def ffn_1(p, s, L):
                yield 2
                n, i, b = halves_index(p, s, L)
                wait(act, "f_xt_ps", n)
                act.activation(at_hi[b][:, :, :], UP[0][:, 0:D].rearrange("p (k t) -> p k t", k=KT), ACT.Copy)\
                   .then_inc(S["f_at_hi"], 1)
                if L == 0:
                    for c in range(2):
                        yield (5, 11)[c]
                        wait(act, f"f_g{c}", i if c else n)
                        act.activation(sg[b][:, CH * c:CH * (c + 1)], UP[0][:, :], ACT.Silu)\
                           .then_inc(S[f"f_sg{c}"], 1)
                        yield (9, 14)[c]
                        wait(act, f"f_h{c}", i if c else n)
                        act.activation(sg[b][:, CH * c:CH * (c + 1)], hid[b][:, CH * c:CH * (c + 1)], ACT.Abs)\
                           .then_inc(S[f"f_abs{c}"], 1)
                else:
                    yield 3
                    wait(act, "f_ro", i)
                    act.activation(rt[:, 0, :], UP[1][:, 0:E], ACT.Abs)
                    act.activation(rt[:, 7, :], UP[1][:, 0:E], ACT.Relu).then_inc(S["f_lg"], 1)
                    yield 5
                    wait(act, "f_lg", i)
                    act.activation(rt[:, 1, :], rt[:, 0, :], ACT.Exp, scale=-1.0).then_inc(S["f_r2"], 1)
                    yield 8
                    wait(act, "f_r3", i)
                    act.activation(rt[:, 3, :], rt[:, 2, :], ACT.Ln).then_inc(S["f_r4"], 1)
                    wait(act, "f_sh", i)
                    act.activation(sg[b][:, 2 * PAIR:2 * PAIR + EI], UP[0][:, 0:EI], ACT.Silu)\
                       .then_inc(S["f_sgs"], 1)
                    yield 12
                    wait(act, "f_g0", n)
                    act.activation(sg[b][:, 0:PAIR], UP[0][:, 0:PAIR], ACT.Silu).then_inc(S["f_sg0"], 1)

            def hidden_t(n, t, b, cols):
                wait(act, f"f_t{t}", n)
                act.activation(ht_hi[:, 4 * t:4 * t + cols // P, :],
                               DOWN[b][:, 0:cols].rearrange("p (k t) -> p k t", t=P), ACT.Copy)\
                   .then_inc(S[f"f_th{t}"], 1)

            def ffn_2(p, s, L):
                yield 1
                n, i, b = halves_index(p, s, L)
                if L == 0:
                    for t in range(2):
                        yield (2, 6)[t]
                        hidden_t(n, t, 0, 4 * P)
                else:
                    hidden_t(i, 3, 1, P)
                    for q in range(1, 4):
                        yield 4 * q
                        wait(act, f"f_gx{q}", i)
                        r = PAIR * (q % 2)
                        act.activation(sg[b][:, r:r + PAIR], DOWN[0][:, 0:PAIR], ACT.Silu)\
                           .then_inc(S[f"f_sgx{q}"], 1)
                    yield 15
                    for t in range(2):
                        hidden_t(n, t, t, 4 * P)
                    yield 18
                    hidden_t(i, 2, 0, 4 * P)

            rounds(act, (attention_1, attention_2, ffn_1, ffn_2), round_ffn_0_weights)

        @block.tensor
        def _(pe):
            pe.wait_ge(S["c_sel"], 11)
            pe.wait_ge(S["c_mem"], 15)

            def product(o, a_hi, a_lo, w_hi, w_lo, first, last, free=False):
                pe.matmul(o, a_hi, w_hi, start=first, stop=False, skip_group_check=free)
                if w_lo is not None:
                    pe.matmul(o, a_hi, w_lo, start=False, stop=False, skip_group_check=free)
                return pe.matmul(o, a_lo, w_hi, start=False, stop=last, skip_group_check=free)

            def turn(o, src, count):
                for k in range(count):
                    last = pe.transpose(o[:, P * k:P * (k + 1)], src(k), ident[:, :])
                return last

            def attention_1(p, s, L):
                yield 2
                n, i, b = halves_index(p, s, L)
                tiles = G[L] // 4
                step = 8 // G[L]
                if L == 1:
                    wait_before(pe, "a_mclear", i)
                if not (isinstance(n, int) and n == 0):
                    wait_part(pe, "a_r", n - 1, 8)
                wait(pe, "a_q_hi", n)
                wait(pe, "a_q_lo", n)
                if L == 0:
                    turn(QK[0], lambda j: q0a[:, j].rearrange("p g b -> p (g b)"), HPG).then_inc(S["a_qt_ps"], 1)
                else:
                    wait(pe, "a_q_hi2", n)
                    turn(QK[0], lambda j: q1[:, j, 0:4].rearrange("p g b -> p (g b)"), HPG).then_inc(S["a_qt_ps"], 1)
                    turn(QK[1], lambda j: q1[:, j, 4:8].rearrange("p g b -> p (g b)"), HPG).then_inc(S["a_qt_ps2"], 1)
                k_ = (k0a if L == 0 else k1)[b]
                order = [(j, t) for t in range(tiles) for j in range(HPG)]
                for m, (j, t) in enumerate(order):
                    yield 3 + m * step
                    if m == 0:
                        pe.wait_ge((ld_k0 if L == 0 else ld_k1)[b], 16 * 8 * use(p, s))
                        wait(pe, "a_qt", n)
                        if L == 1:
                            wait(pe, "a_qt2", i)
                    if m >= 2:
                        wait_part(pe, "a_r", n, step * (m - 1))
                    pe.matmul(QK[(1 + m) % 2][:, :], qt[b][:, t, P * j:P * (j + 1)],
                              k_[:, 4 * t:4 * t + 4, :].rearrange("p g t -> p (g t)"), start=True, stop=True)\
                      .then_inc(S["a_m"], step)

            def attention_2(p, s, L):
                yield 0
                n, i, b = halves_index(p, s, L)
                tiles = G[L] // 4
                step = 8 // G[L]
                wait_before(pe, "a_out", n)
                wait_part(pe, "a_r", n, 8)
                if L == 0:
                    wait(pe, "a_q_hi2", n)
                    turn(PV[0], lambda j: q0b[:, j].rearrange("p g b -> p (g b)"), HPG).then_inc(S["a_mt_ps"], 1)
                else:
                    turn(PV[0], lambda j: q1[:, j, 0:4].rearrange("p g b -> p (g b)"), HPG).then_inc(S["a_mt_ps"], 1)
                    turn(PV[1], lambda j: q1[:, j, 4:8].rearrange("p g b -> p (g b)"), HPG).then_inc(S["a_mt_ps2"], 1)
                for g in range(G[L]):
                    yield 2 + g * step
                    if g == 0:
                        wait(pe, "a_mt", n)
                        if L == 1:
                            wait(pe, "a_mt2", i)
                    if g >= 2:
                        wait_part(pe, "a_e", n, step * (g - 1))
                    o = PV[g % 2][:, :]
                    if L == 0:
                        pe.matmul(o, k0a[b][:, g, :], qt[b][:, 0, :], start=True, stop=False)
                        last = pe.matmul(o, k0b[b][:, g, :], qt[b][:, 1, :], start=False, stop=True)
                    else:
                        last = pe.matmul(o, k1[b][:, g, :], qt[b][:, g // 4, :], start=True, stop=True)
                    last.then_inc(S["a_s"], step)
                yield 10
                wait(pe, "v0_done" if L == 0 else "v1_done", i)
                vv = v0[b] if L == 0 else v1[s]
                wait_part(pe, "a_e", n, 8)
                for t in range(tiles):
                    for g in range(4):
                        last = pe.matmul(PV[t][BLK * g:BLK * (g + 1), :], vv[:, 4 * t + g, :], pt[:, 4 * t + g, :],
                                         start=True, stop=True)
                    last.then_inc(S["a_pv" if t == 0 else "a_pv2"], 1)
                yield 11
                wait(pe, "a_ot", n)
                turn(PV[1] if L == 0 else PV[0], lambda j: ot[:, 0, P * j:P * (j + 1)], HPG).then_inc(S["a_otT"], 1)
                if L == 1:
                    wait(pe, "a_ot2", i)
                    turn(PV[1], lambda j: ot[:, 1, P * j:P * (j + 1)], HPG).then_inc(S["a_otT2"], 1)
                else:
                    yield 12
                    wait(pe, "a_on", n)
                    turn(PV[0], lambda k: on[:, P * k:P * (k + 1)], KT).then_inc(S["a_onT"], 1)
                    yield 13
                    wait(pe, "a_aohi", i)
                    wait(pe, "a_aolo", i)
                    if isinstance(p, int) and p == 0 and s == 0:
                        pe.wait_ge(S["c_hi"], 2)
                        pe.wait_ge(S["c_lo"], 2)
                    for k in range(KT):
                        last = product(PV[1][:, 0:D], ao_hi[:, k, :], ao_lo[:, k, :], wc_hi[:, k, :], wc_lo[:, k, :],
                                       k == 0, k == KT - 1)
                    last.then_inc(S["a_proj"], 1)

            def gate_or_up(o, b, q, off, name):
                for k in range(KT):
                    w = w13_r[:, k, 2 * PAIR * q + off:2 * PAIR * q + off + PAIR]
                    last = product(o[:, 0:PAIR], at_hi[b][:, k, :], at_lo[b][:, k, :], w, None, k == 0, k == KT - 1)
                last.then_inc(S[name + ("0" if q == 0 else f"x{q}")], 1)

            def ffn_1(p, s, L):
                yield 1
                n, i, b = halves_index(p, s, L)
                if isinstance(p, int) and p == 0 and s == 0:
                    if L == 0:
                        pe.wait_ge(S["c_hi"], 4)
                        pe.wait_ge(S["c_lo"], 4)
                    else:
                        pe.wait_ge(S["ld_w13"], 16)
                if s if L == 0 else not s:
                    wait(pe, "f_h1", i - 1 if L == 0 else NS * p + NS - 1)
                else:
                    wait_before(pe, "f_h0", n)
                wait(pe, "f_norm", n)
                turn(UP[0], lambda k: f_xn[:, P * k:P * (k + 1)], KT).then_inc(S["f_xt_ps"], 1)
                yield 3
                wait(pe, "f_at_hi", n)
                wait(pe, "f_at_lo", n)
                if L == 0:
                    for c in range(2):
                        yield (3, 7)[c]
                        for b_, off, name in ((0, 0, "f_g"), (1, I0, "f_u")):
                            if b_:
                                yield (4, 8)[c]
                            if c:
                                wait(pe, "f_h0" if b_ else "f_sg0", n)
                            for k in range(KT):
                                w = slice(off + CH * c, off + CH * (c + 1))
                                last = product(UP[b_][:, :], at_hi[b][:, k, :], at_lo[b][:, k, :],
                                               up_hi[:, k, w], up_lo[:, k, w], k == 0, k == KT - 1)
                            last.then_inc(S[f"{name}{c}"], 1)
                else:
                    for k in range(KT):
                        last = product(UP[1][:, 0:E], at_hi[b][:, k, :], at_lo[b][:, k, :], gate_hi[:, k, :],
                                       gate_lo[:, k, :], k == 0, k == KT - 1)
                    last.then_inc(S["f_ro"], 1)
                    yield 4
                    c0 = 2 * E * EI
                    for k in range(KT):
                        last = product(UP[0][:, 0:2 * EI], at_hi[b][:, k, :], at_lo[b][:, k, :],
                                       w13_r[:, k, c0:c0 + 2 * EI], None, k == 0, k == KT - 1)
                    last.then_inc(S["f_sh"], 1)
                    yield 7
                    wait(pe, "f_lg", i)
                    gate_or_up(UP[1], b, 0, PAIR, "f_u")
                    yield 11
                    wait(pe, "f_hs", i)
                    gate_or_up(UP[0], b, 0, 0, "f_g")

            def ffn_2(p, s, L):
                yield 0
                n, i, b = halves_index(p, s, L)

                if isinstance(p, int) and p == 0 and s == 0:
                    if L == 0:
                        pe.wait_ge(S["c_hi"], 5)
                        pe.wait_ge(S["c_lo"], 5)
                    else:
                        pe.wait_ge(S["ld_w2"], 32)

                def down(ks, w_hi, w_lo, first, last_):
                    for k in ks:
                        last = product(DOWN[1][:, 0:D], ht_hi[:, k, :], ht_lo[:, k, :], w_hi[:, k, :],
                                       None if w_lo is None else w_lo[:, k, :], k == first, k == last_)
                    return last

                if L == 0:
                    for c in range(2):
                        yield (1, 5)[c]
                        wait(pe, f"f_hm{c}", i)
                        if c:
                            wait(pe, "f_th0", n)
                            wait(pe, "f_tl0", n)
                        else:
                            wait_before(pe, "f_out", n)
                        turn(DOWN[0], lambda k: hid[b][:, CH * c + P * k:CH * c + P * (k + 1)], 4)\
                            .then_inc(S[f"f_t{c}"], 1)
                        if c:
                            yield 6
                            down(range(0, 4), down_hi, down_lo, 0, I0 // P - 1)
                            yield 8
                            wait(pe, "f_th1", n)
                            wait(pe, "f_tl1", n)
                            down(range(4, 8), down_hi, down_lo, 0, I0 // P - 1).then_inc(S["f_y"], 1)
                else:
                    def turn_hidden(t, b_, count, m):
                        turn(DOWN[b_], lambda k: hid[b][:, CH * t + P * k:CH * t + P * (k + 1)], count)\
                            .then_inc(S[f"f_t{t}"], 1)

                    wait_before(pe, "f_out", n)
                    wait(pe, "f_hs", i)
                    turn_hidden(3, 1, 1, i)
                    yield 2
                    for q in range(1, 4):
                        yield 4 * q - 2
                        if q > 1:
                            wait(pe, f"f_sgx{q - 1}", i)
                        gate_or_up(DOWN[0], b, q, 0, "f_g")
                        yield 4 * q - 1
                        if q == 1:
                            wait(pe, "f_th3", i)
                            wait(pe, "f_tl3", i)
                        else:
                            wait(pe, f"f_hx{q - 1}", i)
                        gate_or_up(DOWN[1], b, q, PAIR, "f_u")
                    yield 14
                    wait(pe, "f_hx3", i)
                    turn_hidden(0, 0, 4, n)
                    turn_hidden(1, 1, 4, n)
                    yield 17
                    wait(pe, "f_th0", n)
                    wait(pe, "f_tl0", n)
                    turn_hidden(2, 0, 4, i)
                    wait(pe, "f_th1", n)
                    wait(pe, "f_tl1", n)
                    down([NT1 - 1, *range(8)], w2_r, None, NT1 - 1, NT1 - 2)
                    yield 19
                    wait(pe, "f_th2", i)
                    wait(pe, "f_tl2", i)
                    down(range(8, 12), w2_r, None, NT1 - 1, NT1 - 2).then_inc(S["f_y"], 1)

            rounds(pe, (attention_1, attention_2, ffn_1, ffn_2))

        @block.vector
        def _(dve):
            dve.wait_ge(S["c_kh"], 1)
            dve.tensor_tensor(kl, kt_raw, kh.bitcast(F32), ALU.subtract).then_inc(S["c_kl"], 1)
            for s in range(2):
                dve.memset(k0a[s][:, :, :].bitcast(F32), 0.0).then_inc(S["c_oh"], 1)
            dve.wait_ge(S["c_sel"], 3)
            for s in range(2):
                one_hot = [pt[:, h, :].rearrange("p (g t) -> p g t", g=4) for h in (0, 2)]
                dve.tensor_copy(k0b[s][:, :, :], one_hot[0]).then_inc(S["c_oh"], 1)
                for t in range(2):
                    last = dve.tensor_copy(k1[s][:, 4 * t:4 * t + 4, :], one_hot[1])
                last.then_inc(S["c_oh"], 1)
            dve.wait_ge(S["c_tg"], 1)
            dve.tensor_scalar(bcg[:, :], bcg[:, :], tg[:, 0:1], None, ALU.mult).then_inc(S["c_vec"], 1)
            dve.wait_ge(S["c_hi"], 2)
            dve.tensor_tensor(gate_lo[:, :, :], gate_raw[:, :, :], gate_hi[:, :, :].bitcast(F32), ALU.subtract)\
               .then_inc(S["c_lo"], 1)
            dve.tensor_tensor(wc_lo[:, :, :], wc_raw,
                              wc_hi[:, :, :].bitcast(F32), ALU.subtract).then_inc(S["c_lo"], 1)

            def split_ffn_0_weights(t):
                if t == 0:
                    for k in range(KT):
                        dve.wait_ge(S["c_hi"], 3 + k)
                        dve.tensor_tensor(up_lo[:, k, :], up_raw[k], up_hi[:, k, :].bitcast(F32), ALU.subtract)\
                           .then_inc(S["c_lo"], 1)
                    dve.wait_ge(S["c_lo"], 4)
                    for b in range(2):
                        dve.memset(hid[b][:, I1:HW], 0.0).then_inc(S["c_vec"], 1)
                if t == 2:
                    dve.wait_ge(S["c_hi"], 5)
                    dve.tensor_tensor(down_lo[:, :, :], down_raw, down_hi[:, :, :].bitcast(F32), ALU.subtract)\
                       .then_inc(S["c_lo"], 1)

            def norm(pre, n, src, stat, mv, rs, xn):
                dve.bn_stats(stat[:, :], src[:, :]).then_inc(S[pre + "stats"], 1)
                wait_alone(dve, pre + "stats", n)
                dve.bn_aggr(mv[:, :], stat[:, :]).then_inc(S[pre + "mvd"], 1)

            def norm_apply(pre, n, src, mv, rs, xn):
                wait(dve, pre + "rstd", n)
                dve.tensor_scalar(xn[:, :], src[:, :], mv[:, 0:1], rs[:, :], ALU.subtract, ALU.mult)\
                   .then_inc(S[pre + "norm"], 1)

            def attention_1(p, s, L):
                yield 0
                n, i, b = halves_index(p, s, L)
                if L == 0:
                    src = x0[b]
                    dve.wait_ge(ld_x[b], 16 * use(p, s))
                else:
                    src = xr[s]
                    wait(dve, "f_out", n - NS)
                norm("a_", n, src, a_stat, a_mv, a_rs, a_xn)
                yield 1
                wait_before(dve, "a_q_lo", n)
                wait_before(dve, "a_q_hi2", n)
                norm_apply("a_", n, src, a_mv, a_rs, a_xn)
                step = 8 // G[L]
                order = [(j, t) for t in range(G[L] // 4) for j in range(HPG)]
                for m, (j, t) in enumerate(order):
                    yield 3 + m * step
                    wait_part(dve, "a_m", n, step * (m + 1))
                    if L == 0:
                        o = q0b[:, j, :, HD0:HD0 + 1].rearrange("p g o -> p (g o)")
                    else:
                        o = q1[:, j, 4 * t:4 * t + 4, 3 * HD1:3 * HD1 + 1].rearrange("p g o -> p (g o)")
                    dve.tensor_reduce(o, QK[(1 + m) % 2][:, :].rearrange("p (g t) -> p g t", t=T), AX.X, ALU.max,
                                      negate=True).then_inc(S["a_r"], step)

            def attention_2(p, s, L):
                yield 11
                n, i, b = halves_index(p, s, L)
                d = HD[L]
                for t in range(G[L] // 4):
                    wait(dve, "a_otT" if t == 0 else "a_otT2", n if t == 0 else i)
                    o = (PV[1] if L == 0 else PV[t])[:, :].rearrange("p (j g b) -> p j g b", j=HPG, g=4)
                    r = rec[:, :, 4 * t:4 * t + 4]
                    dve.reciprocal(r, o[:, :, :, d:d + 1].rearrange("p j g o -> p j (g o)"))\
                       .then_inc(S["a_rec" if t == 0 else "a_rec2"], 1)
                    wait(dve, "a_rec" if t == 0 else "a_rec2", n if t == 0 else i)
                    ov = on[:, :].rearrange("p (g j d) -> p j g d", g=G[L], j=HPG)[:, :, 4 * t:4 * t + 4, :]
                    dve.tensor_tensor(ov, o[:, :, :, 0:d], r.unsqueeze(3).broadcast_to([P, HPG, 4, d]), ALU.mult)\
                       .then_inc(S["a_on" if t == 0 else "a_on2"], 1)
                if L == 0:
                    yield 12
                    wait(dve, "a_aohi", i)
                    dve.tensor_tensor(ao_lo[:, :, :], PV[0][:, 0:D].rearrange("p (k t) -> p k t", k=KT),
                                      ao_hi[:, :, :].bitcast(F32), ALU.subtract).then_inc(S["a_aolo"], 1)
                    yield 14
                    wait(dve, "a_proj", i)
                    wait(dve, "xb_done", i)
                    dve.scalar_tensor_tensor(out=xr[s][:, :], in0=PV[1][:, 0:D], scalar=tg[:, 0:1], in1=xr[s][:, :],
                                             op0=ALU.mult, op1=ALU.add).then_inc(S["a_out"], 1)
                else:
                    yield 14
                    wait(dve, "a_on2", i)
                    dve.scalar_tensor_tensor(out=xr[s][:, :], in0=on[:, :], scalar=tg[:, 1:2], in1=xr[s][:, :],
                                             op0=ALU.mult, op1=ALU.add).then_inc(S["a_out"], 1)

            def expert_pair(o, b, q, m, x=""):
                wait(dve, f"f_sg{x}{q}", m)
                wait(dve, f"f_u{x}{q}", m)
                for k in range(2):
                    e = 2 * q + k
                    r = PAIR * (q % 2) + EI * k
                    last = dve.scalar_tensor_tensor(
                        out=hid[b][:, EI * e:EI * (e + 1)], in0=o[:, EI * k:EI * (k + 1)],
                        scalar=cw[b][:, e:e + 1], in1=sg[b][:, r:r + EI], op0=ALU.mult, op1=ALU.mult)
                last.then_inc(S[f"f_h{x}{q}"], 1)

            def sparsify(c, n, i, b, last_step):
                cols = slice(CH * c, CH * (c + 1))
                if c:
                    wait(dve, "f_keep0", i)
                else:
                    wait_before(dve, "f_keep1", i)
                wait(dve, f"f_abs{c}", i)
                a = sg[b][:, cols].rearrange("p (n a e) -> p n a e", a=2, e=2)
                dve.tensor_tensor(lose[:, :, :, 0], a[:, :, :, 0], a[:, :, :, 1], ALU.is_lt)\
                   .then_inc(S[f"f_first{c}"], 1)
                dve.tensor_tensor(pmax[:, :, :], a[:, :, :, 0], a[:, :, :, 1], ALU.max)
                dve.tensor_tensor(pmin[:, :, :], a[:, :, :, 0], a[:, :, :, 1], ALU.min)\
                   .then_inc(S[f"f_pairs{c}"], 1)
                wait(dve, f"f_pairs{c}", i)
                dve.tensor_tensor(both[:, 0, :], pmin[:, :, 0], pmax[:, :, 1], ALU.is_ge)
                dve.tensor_tensor(both[:, 1, :], pmin[:, :, 1], pmax[:, :, 0], ALU.is_gt)\
                   .then_inc(S[f"f_cmp{c}"], 1)
                yield last_step
                wait(dve, f"f_lead{c}", i)
                dve.tensor_tensor(keep[:, c, :].rearrange("p (n a e) -> p n a e", a=2, e=2),
                                  lead[:, :, :].unsqueeze(3).broadcast_to([P, NG, 2, 2]), lose[:, :, :, :],
                                  ALU.is_ge).then_inc(S[f"f_keep{c}"], 1)

            def ffn_1(p, s, L):
                yield 0
                n, i, b = halves_index(p, s, L)
                src = xr[s]
                wait(dve, "a_out", n)
                norm("f_", n, src, f_stat, f_mv, f_rs, f_xn)
                yield 1
                norm_apply("f_", n, src, f_mv, f_rs, f_xn)
                yield 2
                wait(dve, "f_at_hi", n)
                dve.tensor_tensor(at_lo[b][:, :, :], UP[0][:, 0:D].rearrange("p (k t) -> p k t", k=KT),
                                  at_hi[b][:, :, :].bitcast(F32), ALU.subtract).then_inc(S["f_at_lo"], 1)
                if L == 0:
                    for c in range(2):
                        yield (6, 12)[c]
                        cols = slice(CH * c, CH * (c + 1))
                        wait(dve, f"f_sg{c}", i if c else n)
                        wait(dve, f"f_u{c}", i if c else n)
                        dve.tensor_tensor(hid[b][:, cols], UP[1][:, :], sg[b][:, cols], ALU.mult)\
                           .then_inc(S[f"f_h{c}"], 1)
                        if c == 0:
                            yield 10
                            keep_0 = sparsify(0, n, i, b, 13)
                            next(keep_0)
                    yield 13
                    next(keep_0, None)
                else:
                    yield 10
                    wait(dve, "f_sgs", i)
                    dve.tensor_tensor(hid[b][:, E * EI:I1], UP[0][:, EI:2 * EI], sg[b][:, 2 * PAIR:2 * PAIR + EI],
                                      ALU.mult)\
                       .then_inc(S["f_hs"], 1)
                    yield 13
                    wait(dve, "f_r11", i)
                    own = rt[:, 9, :].unsqueeze(2).broadcast_to([P, E, E])
                    other = rt[:, 9, :].unsqueeze(1).broadcast_to([P, E, E])
                    dve.tensor_tensor(cmp[:, 0], other, own, ALU.is_ge)
                    dve.tensor_tensor(cmp[:, 1], other, own, ALU.is_gt).then_inc(S["f_cmp2"], 1)
                    wait(dve, "f_cmp2", i)
                    dve.tensor_tensor(cmp[:, :, :, :], cmp[:, :, :, :], tie[:, :, :, :], ALU.mult)\
                       .then_inc(S["f_cmp3"], 1)
                    wait(dve, "f_cmp3", i)
                    dve.tensor_reduce(rank[:, :], cmp[:, :, :, :].rearrange("p a e f -> p e a f"), AX.XY, ALU.add)\
                       .then_inc(S["f_rank"], 1)
                    wait(dve, "f_rank", i)
                    dve.scalar_tensor_tensor(out=cw[b][:, :], in0=rank[:, :], scalar=1.5, in1=rt[:, 8, :],
                                             op0=ALU.is_lt, op1=ALU.mult).then_inc(S["f_cw"], 1)
                    yield 14
                    wait(dve, "f_cw", i)
                    expert_pair(UP[1], b, 0, n)

            def hidden_t(n, t, b, cols):
                wait(dve, f"f_th{t}", n)
                r = slice(4 * t, 4 * t + cols // P)
                dve.tensor_tensor(ht_lo[:, r, :], DOWN[b][:, 0:cols].rearrange("p (k t) -> p k t", t=P),
                                  ht_hi[:, r, :].bitcast(F32), ALU.subtract).then_inc(S[f"f_tl{t}"], 1)

            def ffn_2(p, s, L):
                yield 0
                n, i, b = halves_index(p, s, L)
                if L == 0:
                    yield 0
                    yield from sparsify(1, n, i, b, 3)
                    for t in range(2):
                        yield (4, 7)[t]
                        hidden_t(n, t, 0, 4 * P)
                    yield 9
                    wait(dve, "f_y", n)
                    dve.scalar_tensor_tensor(out=xr[s][:, :], in0=DOWN[1][:, 0:D], scalar=tg[:, 2:3], in1=xr[s][:, :],
                                             op0=ALU.mult, op1=ALU.add).then_inc(S["f_out"], 1)
                else:
                    yield 1
                    hidden_t(i, 3, 1, P)
                    for q in range(1, 4):
                        yield 4 * q + 1
                        expert_pair(DOWN[1], b, q, i, "x")
                    yield 16
                    for t in range(2):
                        hidden_t(n, t, t, 4 * P)
                    yield 18
                    hidden_t(i, 2, 0, 4 * P)
                    yield 20
                    wait(dve, "f_y", n)
                    if not (isinstance(p, int) and p + s == 0):
                        dve.wait_ge(st_y, 16 * i)
                    dve.scalar_tensor_tensor(out=y[:, :], in0=DOWN[1][:, 0:D], scalar=tg[:, 3:4], in1=xr[s][:, :],
                                             op0=ALU.mult, op1=ALU.add).then_inc(S["f_out"], 1)

            rounds(dve, (attention_1, attention_2, ffn_1, ffn_2), split_ffn_0_weights)


_IN = ["x", "ctx_kv", "ctx_t", "g_x", "g_f", "wc_t", "bc", "w_up", "w_down", "gate_w_t", "gate_b", "w13", "w2"]


def kernel(x, ctx_512, g_xattn, g_ffn, L0_xattn_Wc, L0_xattn_bc, L0_ffn_w_gate, L0_ffn_w_up, L0_ffn_w_down,
           L1_ffn_gate_w, L1_ffn_gate_b, L1_ffn_w1, L1_ffn_w2, L1_ffn_w3, L1_ffn_sw1, L1_ffn_sw2, L1_ffn_sw3):
    import concourse.bacc as bacc
    from concourse.bass_utils import run_bass_kernel_spmd

    E, EI, D = L1_ffn_w1.shape
    up = []
    for q in range(E // 2):
        up += [L1_ffn_w1[2 * q], L1_ffn_w1[2 * q + 1], L1_ffn_w3[2 * q], L1_ffn_w3[2 * q + 1]]
    w13 = np.concatenate(up + [L1_ffn_sw1, L1_ffn_sw3], axis=0).T
    w2 = np.concatenate([L1_ffn_w2.transpose(0, 2, 1).reshape(E * EI, D), np.asarray(L1_ffn_sw2).T], axis=0)
    arrays = {
        "x": x, "ctx_kv": ctx_512, "ctx_t": ctx_512.transpose(2, 0, 1).reshape(ctx_512.shape[2], -1),
        "g_x": g_xattn, "g_f": g_ffn, "wc_t": L0_xattn_Wc.T, "bc": L0_xattn_bc,
        "w_up": np.concatenate([L0_ffn_w_gate, L0_ffn_w_up], axis=1), "w_down": L0_ffn_w_down,
        "gate_w_t": L1_ffn_gate_w.T, "gate_b": L1_ffn_gate_b, "w13": w13, "w2": w2,
    }
    arrays = {f"in_{k}": np.ascontiguousarray(v) for k, v in arrays.items()}
    nc = bacc.Bacc("TRN2", target_bir_lowering=False, num_devices=1)
    args = [nc.dram_tensor(f"in_{k}", arrays[f"in_{k}"].shape, mybir.dt.from_np(arrays[f"in_{k}"].dtype),
                           kind="ExternalInput").ap() for k in _IN]
    out = nc.dram_tensor("out", arrays["in_x"].shape, F32, kind="ExternalOutput").ap()
    flamingo_block(nc, *args, out)
    return run_bass_kernel_spmd(nc, [arrays], core_ids=[0]).results[0]["out"]
```
